# Optimizing a Trainium2 kernel written in Bass

```python
import numpy as np
import jax
import jax.numpy as jnp

def _softmax(x, axis=-1):
    return jax.nn.softmax(x, axis=axis)

def _gelu(x):
    return jax.nn.gelu(x, approximate=True)

def _silu(x):
    return jax.nn.silu(x)

def _sigmoid(x):
    return jax.nn.sigmoid(x)

def _layernorm(x, axis=-1, eps=1e-05):
    m = jnp.mean(x, axis=axis, keepdims=True)
    v = jnp.var(x, axis=axis, keepdims=True)
    return (x - m) / jnp.sqrt(v + eps)

def _scatter_add(tgt, idx, src, axis=0):
    return tgt.at[idx].add(src)

def _segment_sum(src, seg, n):
    return jax.ops.segment_sum(src, seg, n)
kernel_name = 'mk_gnn_preln_d1_gnn_r8_2bd89c'

def setup_inputs(seed: int=0):
    np.random.seed(seed)
    _w = jnp.asarray

    def _rec_inputs():
        import jax
        import jax.numpy as jnp
        _gk = jax.random.key(seed)
        x = -0.000202 + 1 * jax.random.normal(jax.random.fold_in(_gk, 1), (6250, 128), jnp.float32)
        src = jax.random.randint(jax.random.fold_in(_gk, 2), (200000,), 0, 6250, jnp.int32)
        dst = jnp.minimum((6250 * jax.random.uniform(jax.random.fold_in(_gk, 3), (200000,)) ** 2.0).astype(jnp.int32), 49999)
        _o = jnp.argsort(dst, stable=True)
        src = src[_o]
        dst = dst[_o]
        edge_attr_4 = -0.0005303 + 1.00001 * jax.random.normal(jax.random.fold_in(_gk, 12), (200000, 4), jnp.float32)
        edge_weight = jax.random.uniform(jax.random.fold_in(_gk, 13), (200000,), jnp.float32, 0.0, 5.99999)
        node_vec1 = jax.random.uniform(jax.random.fold_in(_gk, 14), (6250, 1), jnp.float32, 0.0, 1)
        return (x, src, dst, edge_attr_4, edge_weight, node_vec1)
    x, src, dst, edge_attr_4, edge_weight, node_vec1 = _rec_inputs()

    def _L0_gnn_setup():
        import jax, jax.numpy as jnp
        import numpy as np
        N_NODES = 6250
        N_EDGES = 62500
        MUL = 32
        NUM_RBF = 8
        CUTOFF = 6.0

        def _forward(node_input, node_attr, edge_sh_attr, edge_scalar_distances, edge_src, edge_dst, sc_ws, sc_wv, lin1_ws, lin1_wv, fc_w1, fc_w2, fc_w3, lin2_ws, lin2_wv, alpha_w):
            N = node_input.shape[0]
            dt = node_input.dtype
            d = edge_scalar_distances[:, None]
            freqs = jnp.arange(1, NUM_RBF + 1, dtype=dt) * (jnp.pi / CUTOFF)
            fd = d * freqs
            small = jnp.abs(fd) < 1e-06
            safe_fd = jnp.where(small, jnp.ones_like(fd), fd)
            rbf = jnp.where(small, jnp.ones_like(fd), jnp.sin(safe_fd) / safe_fd)
            cut = (d <= CUTOFF).astype(dt) * (0.5 * (jnp.cos(jnp.pi * d / CUTOFF) + 1.0))
            rbf = cut * rbf
            h = jax.nn.silu(rbf @ fc_w1 / jnp.sqrt(jnp.asarray(NUM_RBF, dt)))
            h = jax.nn.silu(h @ fc_w2 / jnp.sqrt(jnp.asarray(64.0, dt)))
            weight = h @ fc_w3 / jnp.sqrt(jnp.asarray(64.0, dt))
            w00, w01, w10, w11 = jnp.split(weight, 4, axis=1)
            x_s = node_input[:, :MUL]
            x_v = node_input[:, MUL:].reshape(N, MUL, 3)
            a = node_attr

            def fctp(xs, xv, ws, wv, n_in):
                inv = 1.0 / jnp.sqrt(jnp.asarray(n_in, dt))
                s = xs @ ws * a * inv
                v = jnp.einsum('nim,io->nom', xv, wv) * a[:, :, None] * inv
                return (s, v)
            sc_s, sc_v = fctp(x_s, x_v, sc_ws, sc_wv, MUL)
            l1_s, l1_v = fctp(x_s, x_v, lin1_ws, lin1_wv, MUL)
            gs = l1_s[edge_src]
            gv = l1_v[edge_src]
            sh0 = edge_sh_attr[:, 0:1]
            sh1 = edge_sh_attr[:, 1:4]
            o00 = w00 * gs * sh0
            o01 = w01[:, :, None] * gs[:, :, None] * sh1[:, None, :]
            o10 = w10[:, :, None] * gv * sh0[:, :, None]
            o11 = w11 * (jnp.einsum('ecm,em->ec', gv, sh1) / jnp.sqrt(jnp.asarray(3.0, dt)))
            msg_s = jnp.concatenate([o00, o11], axis=1)
            msg_v = jnp.concatenate([o01, o10], axis=1)
            cnt = jax.ops.segment_sum(jnp.ones((edge_dst.shape[0],), dt), edge_dst, num_segments=N)
            cnt = jnp.clip(cnt, 1.0)[:, None]
            agg_s = jax.ops.segment_sum(msg_s, edge_dst, num_segments=N) / cnt
            agg_v = jax.ops.segment_sum(msg_v, edge_dst, num_segments=N) / cnt[:, :, None]
            inv2 = 1.0 / jnp.sqrt(jnp.asarray(2 * MUL, dt))
            l2_s = agg_s @ lin2_ws * a * inv2
            l2_v = jnp.einsum('nim,io->nom', agg_v, lin2_wv) * a[:, :, None] * inv2
            alpha = jnp.tanh(agg_s @ alpha_w * a * inv2)
            out_s = sc_s + alpha * l2_s
            out_v = sc_v + alpha[:, :, None] * l2_v
            return jnp.concatenate([out_s, out_v.reshape(N, 3 * MUL)], axis=1)
        key = jax.random.key(seed)
        ks = jax.random.split(key, 16)
        f = jnp.float32
        return {'node_input': jax.random.normal(ks[0], (N_NODES, 4 * MUL), dtype=f), 'node_attr': jnp.ones((N_NODES, 1), dtype=f), 'edge_sh_attr': jax.random.normal(ks[1], (N_EDGES, 4), dtype=f), 'edge_scalar_distances': jax.random.uniform(ks[2], (N_EDGES,), dtype=f, minval=0.1, maxval=CUTOFF), 'edge_src': jax.random.randint(ks[3], (N_EDGES,), 0, N_NODES, dtype=jnp.int32), 'edge_dst': jax.random.randint(ks[4], (N_EDGES,), 0, N_NODES, dtype=jnp.int32), 'sc_ws': jax.random.normal(ks[5], (MUL, MUL), dtype=f), 'sc_wv': jax.random.normal(ks[6], (MUL, MUL), dtype=f), 'lin1_ws': jax.random.normal(ks[7], (MUL, MUL), dtype=f), 'lin1_wv': jax.random.normal(ks[8], (MUL, MUL), dtype=f), 'fc_w1': jax.random.normal(ks[9], (NUM_RBF, 64), dtype=f), 'fc_w2': jax.random.normal(ks[10], (64, 64), dtype=f), 'fc_w3': jax.random.normal(ks[11], (64, 4 * MUL), dtype=f), 'lin2_ws': jax.random.normal(ks[12], (2 * MUL, MUL), dtype=f), 'lin2_wv': jax.random.normal(ks[13], (2 * MUL, MUL), dtype=f), 'alpha_w': jax.random.normal(ks[14], (2 * MUL, 1), dtype=f) * 0.1}
    _L0_gnn_all = _L0_gnn_setup()
    _L0_gnn_in = {k: v for k, v in _L0_gnn_all.items() if k in ('sc_ws', 'sc_wv', 'lin1_ws', 'lin1_wv', 'fc_w1', 'fc_w2', 'fc_w3', 'lin2_ws', 'lin2_wv', 'alpha_w')}
    del _L0_gnn_all
    return {'x': x, 'src': src, 'dst': dst, 'edge_attr_4': edge_attr_4, 'edge_weight': edge_weight, 'node_vec1': node_vec1, 'L0_gnn_sc_ws': _L0_gnn_in['sc_ws'], 'L0_gnn_sc_wv': _L0_gnn_in['sc_wv'], 'L0_gnn_lin1_ws': _L0_gnn_in['lin1_ws'], 'L0_gnn_lin1_wv': _L0_gnn_in['lin1_wv'], 'L0_gnn_fc_w1': _L0_gnn_in['fc_w1'], 'L0_gnn_fc_w2': _L0_gnn_in['fc_w2'], 'L0_gnn_fc_w3': _L0_gnn_in['fc_w3'], 'L0_gnn_lin2_ws': _L0_gnn_in['lin2_ws'], 'L0_gnn_lin2_wv': _L0_gnn_in['lin2_wv'], 'L0_gnn_alpha_w': _L0_gnn_in['alpha_w']}

def reference(x, src, dst, edge_attr_4, edge_weight, node_vec1, L0_gnn_sc_ws, L0_gnn_sc_wv, L0_gnn_lin1_ws, L0_gnn_lin1_wv, L0_gnn_fc_w1, L0_gnn_fc_w2, L0_gnn_fc_w3, L0_gnn_lin2_ws, L0_gnn_lin2_wv, L0_gnn_alpha_w):
    import jax
    import jax.numpy as jnp

    def _L0_gnn_ref(node_input, node_attr, edge_sh_attr, edge_scalar_distances, edge_src, edge_dst, sc_ws, sc_wv, lin1_ws, lin1_wv, fc_w1, fc_w2, fc_w3, lin2_ws, lin2_wv, alpha_w):
        import jax, jax.numpy as jnp
        import numpy as np
        N_NODES = 6250
        N_EDGES = 62500
        MUL = 32
        NUM_RBF = 8
        CUTOFF = 6.0

        def _forward(node_input, node_attr, edge_sh_attr, edge_scalar_distances, edge_src, edge_dst, sc_ws, sc_wv, lin1_ws, lin1_wv, fc_w1, fc_w2, fc_w3, lin2_ws, lin2_wv, alpha_w):
            N = node_input.shape[0]
            dt = node_input.dtype
            d = edge_scalar_distances[:, None]
            freqs = jnp.arange(1, NUM_RBF + 1, dtype=dt) * (jnp.pi / CUTOFF)
            fd = d * freqs
            small = jnp.abs(fd) < 1e-06
            safe_fd = jnp.where(small, jnp.ones_like(fd), fd)
            rbf = jnp.where(small, jnp.ones_like(fd), jnp.sin(safe_fd) / safe_fd)
            cut = (d <= CUTOFF).astype(dt) * (0.5 * (jnp.cos(jnp.pi * d / CUTOFF) + 1.0))
            rbf = cut * rbf
            h = jax.nn.silu(rbf @ fc_w1 / jnp.sqrt(jnp.asarray(NUM_RBF, dt)))
            h = jax.nn.silu(h @ fc_w2 / jnp.sqrt(jnp.asarray(64.0, dt)))
            weight = h @ fc_w3 / jnp.sqrt(jnp.asarray(64.0, dt))
            w00, w01, w10, w11 = jnp.split(weight, 4, axis=1)
            x_s = node_input[:, :MUL]
            x_v = node_input[:, MUL:].reshape(N, MUL, 3)
            a = node_attr

            def fctp(xs, xv, ws, wv, n_in):
                inv = 1.0 / jnp.sqrt(jnp.asarray(n_in, dt))
                s = xs @ ws * a * inv
                v = jnp.einsum('nim,io->nom', xv, wv) * a[:, :, None] * inv
                return (s, v)
            sc_s, sc_v = fctp(x_s, x_v, sc_ws, sc_wv, MUL)
            l1_s, l1_v = fctp(x_s, x_v, lin1_ws, lin1_wv, MUL)
            gs = l1_s[edge_src]
            gv = l1_v[edge_src]
            sh0 = edge_sh_attr[:, 0:1]
            sh1 = edge_sh_attr[:, 1:4]
            o00 = w00 * gs * sh0
            o01 = w01[:, :, None] * gs[:, :, None] * sh1[:, None, :]
            o10 = w10[:, :, None] * gv * sh0[:, :, None]
            o11 = w11 * (jnp.einsum('ecm,em->ec', gv, sh1) / jnp.sqrt(jnp.asarray(3.0, dt)))
            msg_s = jnp.concatenate([o00, o11], axis=1)
            msg_v = jnp.concatenate([o01, o10], axis=1)
            cnt = jax.ops.segment_sum(jnp.ones((edge_dst.shape[0],), dt), edge_dst, num_segments=N)
            cnt = jnp.clip(cnt, 1.0)[:, None]
            agg_s = jax.ops.segment_sum(msg_s, edge_dst, num_segments=N) / cnt
            agg_v = jax.ops.segment_sum(msg_v, edge_dst, num_segments=N) / cnt[:, :, None]
            inv2 = 1.0 / jnp.sqrt(jnp.asarray(2 * MUL, dt))
            l2_s = agg_s @ lin2_ws * a * inv2
            l2_v = jnp.einsum('nim,io->nom', agg_v, lin2_wv) * a[:, :, None] * inv2
            alpha = jnp.tanh(agg_s @ alpha_w * a * inv2)
            out_s = sc_s + alpha * l2_s
            out_v = sc_v + alpha[:, :, None] * l2_v
            return jnp.concatenate([out_s, out_v.reshape(N, 3 * MUL)], axis=1)
        return _forward(node_input, node_attr, edge_sh_attr, edge_scalar_distances, edge_src, edge_dst, sc_ws, sc_wv, lin1_ws, lin1_wv, fc_w1, fc_w2, fc_w3, lin2_ws, lin2_wv, alpha_w)
    h = jnp.maximum(_layernorm(x, axis=-1), 0.0)
    x = x + _L0_gnn_ref(h, node_vec1, edge_attr_4, edge_weight, src, dst, L0_gnn_sc_ws, L0_gnn_sc_wv, L0_gnn_lin1_ws, L0_gnn_lin1_wv, L0_gnn_fc_w1, L0_gnn_fc_w2, L0_gnn_fc_w3, L0_gnn_lin2_ws, L0_gnn_lin2_wv, L0_gnn_alpha_w)
    return x

_drawn_inputs = setup_inputs


def setup_inputs(seed=0):
    import zlib

    import numpy as np

    out = dict(_drawn_inputs(seed))
    spreads = {}
    factors = {'edge_attr_4': 8.0,
     'edge_weight': 8.0,
     'L0_gnn_lin1_ws': 8.0,
     'L0_gnn_lin1_wv': 8.0,
     'L0_gnn_fc_w1': 8.0,
     'L0_gnn_fc_w2': 8.0,
     'L0_gnn_fc_w3': 8.0,
     'L0_gnn_lin2_ws': 8.0,
     'L0_gnn_lin2_wv': 8.0,
     'L0_gnn_alpha_w': 8.0,
     'L0_gnn_sc_ws': 64.0,
     'L0_gnn_sc_wv': 64.0}
    for name, (base, spread) in spreads.items():
        noise = np.random.default_rng([zlib.crc32(name.encode()), seed]).standard_normal(out[name].shape)
        drawn = base * np.exp(spread * noise) if base else spread * noise
        out[name] = jnp.asarray(drawn.astype(out[name].dtype))
    for name, factor in factors.items():
        out[name] = (out[name] * factor).astype(out[name].dtype)
    return out
```

```python
from contextlib import ExitStack
from math import pi, sqrt

import numpy as np
import concourse.bass as bass
from concourse import mybir

F32 = mybir.dt.float32
I32 = mybir.dt.int32
I16 = mybir.dt.int16
ALU = mybir.AluOpType
ACT = mybir.ActivationFunctionType
AX_X = mybir.AxisListType.X

P = 128
N = 6250
C = 128
E = 200000
MUL = 32
RBF = 8
HID = 64
CUTOFF = 6.0
SMALL = 1e-6
EPS = 1e-5
ROUND = 1.5 * 2.0 ** 23

NBLK = -(-N // P)
BI = 7
NI = NBLK // BI
TAIL = N - (NBLK - 1) * P

ROWS = 125
LEN = E // ROWS
RA = 112
PAD = P
W = 14 * P
STEPS = 11
LCH = W // P

G = 8
NPAIR = G // 2
TILES = -(-E // P)
BODY = 2 * G
NBODY = -(-TILES // BODY)
IDC = 400
NIDC = 4
IDW = IDC * NIDC
REC = 8
SRC, DST, CNT, SH = 1, 2, 3, 4

FC = 3
MSG = FC * P
AGGW = (NBLK + 1) * P + 8
WIN = P


def gnn_kernel(nc, x, src, dst, edge_attr_4, edge_weight, node_vec1, sc_ws, sc_wv, lin1_ws, lin1_wv,
               fc_w1, fc_w2, fc_w3, lin2_ws, lin2_wv, alpha_w, out):
    rec_tab = nc.dram_tensor("rec_tab", (E + 1, REC), F32, kind="Internal").ap()
    l1_tab = nc.dram_tensor("l1_tab", (NBLK * P, C), F32, kind="Internal").ap()

    ctx = ExitStack()
    with ctx:
        def sb(name, shape, dt=F32):
            return ctx.enter_context(nc.sbuf_tensor(name, shape, dt))

        def sem(name):
            return ctx.enter_context(nc.semaphore(name))

        big = sb("big", [P, FC * AGGW])
        rec_rows = big[0:ROWS, 0:(LEN + 1) * REC].rearrange("p (e f) -> p e f", f=REC)
        attr_rows = big[0:ROWS, (LEN + 1) * REC:(LEN + 1) * REC + 4 * LEN]
        at_h = (LEN + 1) * REC
        hbuf = big[:, at_h:at_h + BI * C].rearrange("p (b c) -> p b c", b=BI)
        hT = big[:, at_h + BI * C:at_h + 2 * BI * C].rearrange("p (b c) -> p b c", b=BI)
        lsb = big[:, at_h + 2 * BI * C:at_h + 4 * BI * C].rearrange("p (b c) -> p b c", b=BI)
        agg = big[:, :].rearrange("p (c n) -> p c n", c=FC)

        work = sb("work", [P, 8 * W + 3 * W // 2 + (W + 1024) // 2])

        def col(n, width=W, at=0):
            return work[0:ROWS, n * W + at:n * W + at + width]

        dist, dst_raw, src_raw, dst_f = col(0, LEN), col(1, LEN), col(2, LEN), col(3, LEN + 1)
        place1, rank, last1, listed = col(4, LEN), col(5, LEN), col(6, LEN + 1), col(7, LEN)
        tile_no = col(0, P // 8 + IDW)
        mark1, shift0, tile_hot = dst_raw, dst_raw, col(1, P // 8 + IDW)
        edge_base, edge_no = col(2), col(3)
        at16 = 8 * W
        sh_a = work[0:ROWS, at16:at16 + W // 2].bitcast(I16)
        sh_b = work[0:ROWS, at16 + W // 2:at16 + W].bitcast(I16)
        stay = work[0:ROWS, at16 + W:at16 + 3 * W // 2].bitcast(I16)
        move = work[0:ROWS, at16 + 3 * W // 2:at16 + 3 * W // 2 + (W + 1024) // 2].bitcast(I16)

        used = [0]

        def carve(*shape):
            n = int(np.prod(shape))
            v = work[:, used[0]:used[0] + n]
            used[0] += n
            if len(shape) == 2:
                return v.rearrange("p (a b) -> p a b", a=shape[0])
            if len(shape) == 3:
                return v.rearrange("p (a b c) -> p a b c", a=shape[0], b=shape[1])
            return v

        gath = carve(2, G, C)
        gsh0 = carve(G, C)
        gsh1 = carve(G, 3, MUL)
        t01 = carve(G, MUL)
        dot1, dot2 = carve(G, MUL), carve(G, MUL)
        msg = carve(G, MSG)
        hot = carve(G, WIN)
        aggb = [carve(FC, BI * P), carve(FC, BI * P)]
        assert used[0] <= 8 * W

        base = sb("base", [P, NBLK, C])
        ids = sb("ids", [P, IDW], I32)
        rec, recw = sb("rec", [P, 2, G, REC]), sb("recw", [P, 2, G, REC])
        ids_g, src_g = sb("ids_g", [P, 2, G], I32), sb("src_g", [P, 2, G], I32)
        rbfT, h1, h2 = sb("rbfT", [RBF * G, P]), sb("h1", [P, 4 * P]), sb("h2", [P, 4 * P])
        d6, cosv, cut2, cut = sb("d6", [P, G]), sb("cosv", [P, G]), sb("cut2", [P, G]), sb("cut", [P, G])
        turns, whole, frac = sb("turns", [P, G, RBF]), sb("whole", [P, G, RBF]), sb("frac", [P, G, RBF])
        fd, rfd, sinv = sb("fd", [P, G, RBF]), sb("rfd", [P, G, RBF]), sb("sinv", [P, G, RBF])
        small = sb("small", [P, G, RBF], I32)
        rb, rbf = sb("rb", [P, G, RBF]), sb("rbf", [P, G * RBF])
        dst_c = sb("dst_c", [P, G])
        minmax, diag = sb("minmax", [G, 2]), sb("diag", [G, 2, G])
        win0, winmax, span4 = sb("win0", [P, NPAIR]), sb("winmax", [P, NPAIR]), sb("span4", [P, NPAIR])
        win0_i, span_i = sb("win0_i", [P, NPAIR], I32), sb("span_i", [P, 1], I32)
        dloc = sb("dloc", [P, G])

        ident, iota, tri = sb("ident", [P, P]), sb("iota", [P, WIN]), sb("tri", [P, P])
        ones, half_pi = sb("ones", [P, P]), sb("half_pi", [P, 1])
        kturn, kfreq = sb("kturn", [P, RBF]), sb("kfreq", [P, RBF])
        w1, w2 = sb("w1", [RBF * G, 4, P]), sb("w2", [P, P])
        w3r, w3 = sb("w3r", [P, 2, C]), sb("w3", [P, 2, C])
        wl = sb("wl", [P, 2 * C])
        wsc = sb("wsc", [P, C])
        wagg, wv2 = sb("wagg", [P, 2, C + 1]), sb("wv2", [P, MUL])
        at_rows = sb("at_rows", [NBLK, P])
        a_in, a_agg = sb("a_in", [P, NBLK]), sb("a_agg", [P, NBLK])
        stats, mv7, mv = sb("stats", [P, BI, 6]), sb("mv7", [P, BI, 2]), sb("mv", [P, NBLK, 2])
        std, rstd, nmr = sb("std", [P, NBLK]), sb("rstd", [P, NBLK]), sb("nmr", [P, NBLK])
        base_i, tile0_i, off_i = sb("base_i", [ROWS, 1], I32), sb("tile0_i", [ROWS, 1], I32), sb("off_i", [ROWS, 1], I32)
        tile0_f, off_f, pad_off = sb("tile0_f", [ROWS, 1]), sb("off_f", [ROWS, 1]), sb("pad_off", [ROWS, 1])
        tot_i, nbody = sb("tot_i", [P, 1], I32), sb("nbody", [P, 1], I32)
        none = sb("none", [P, IDC])
        cmax, rcnt, scale = sb("cmax", [P, 2, BI]), sb("rcnt", [P, 2, BI]), sb("scale", [P, 2, BI])
        apre, alpha, salpha = sb("apre", [P, 2, BI]), sb("alpha", [P, 2, BI]), sb("salpha", [P, 2, BI])

        ps = ctx.enter_context(nc.psum_tensor("ps", [P, 8, 512], F32))
        ps_hT = [ps[:, k, 0:C] for k in range(2)]
        ps_l = [ps[:, 2 + k, 0:2 * C] for k in range(4)]
        ps_a, ps_id = ps[:, 6, 0:NBLK], ps[:, 7, 0:IDC]
        ps_start, ps_total = ps[0:ROWS, 7, 0:1], ps[:, 7, 1:2]
        ps_w = [ps[:, 2 * s:2 * s + 2, :].rearrange("p k (t c) -> p (k t) c", c=C) for s in range(2)]
        ps_z, ps_x = ps[:, 4, :], ps[:, 5, :]
        ps_s = [ps[:, 6 + s, 0:MSG].rearrange("p (c n) -> p c n", c=FC) for s in range(2)]
        def ps_e(s, j):
            return ps[:, 3 * s + j // 3, (j % 3) * (C + 1):(j % 3 + 1) * (C + 1)]
        ps_c = [ps[:, 6 + s, 0:BI] for s in range(2)]

        s_x, s_at, s_dist, s_dst, s_src, s_attr = (sem(n) for n in ("x_in", "at_in", "dist_in", "dst_in", "src_in", "attr_in"))
        s_wraw, s_wz, s_tail, s_lfree = sem("weights_in"), sem("weights_zeroed"), sem("tails_zeroed"), sem("l_rows_stored")
        s_const, s_pool, s_dve, s_act = sem("consts"), sem("pool_step"), sem("dve_step"), sem("act_step")
        s_recp, s_reca, s_recd = sem("rec_src_dst"), sem("rec_dist_attr"), sem("rec_cnt")
        s_rtab, s_ltab = sem("rec_tab_written"), sem("l1_tab_written")
        s_atT, s_ain, s_var, s_std, s_norm = (sem(n) for n in ("attr_T", "attr_scaled", "var_ready", "std_ready", "norm_ready"))
        s_h, s_hTp, s_hT, s_lp, s_lsb, s_base = (sem(n) for n in ("h_ready", "hT_psum", "hT_ready", "l_psum", "l_ready", "base_ready"))
        s_wdone = sem("weights_ready")
        s_cnt, s_pre, s_off, s_tno, s_ebase = (sem(n) for n in ("row_counts", "row_starts", "rows_free", "tile_no_ready", "edge_base_ready"))
        s_ln, s_ide2, s_hotid, s_idp, s_ide, s_nb, s_ids = (sem(n) for n in ("ln_turn", "ids_none", "edge_no_ready", "ids_psum", "ids_psum_read", "nbody_ready", "ids_ready"))
        s_agg0 = sem("agg_zeroed")
        s_idg, s_rc = sem("ids_g_ready"), sem("rec_copied")
        s_rec = [sem("rec_in0"), sem("rec_in1")]
        s_gat = [sem("gath_in0"), sem("gath_in1")]
        s_frac, s_sin, s_rbf, s_rT, s_rbfT = (sem(n) for n in ("frac_ready", "sin_ready", "rbf_ready", "rbfT_psum", "rbfT_ready"))
        s_z1, s_h1, s_z2, s_h2, s_w = (sem(n) for n in ("z1_ready", "h1_ready", "z2_ready", "h2_ready", "w_ready"))
        s_diag, s_bc, s_win = sem("diag_ready"), sem("windows_psum"), sem("windows_ready")
        s_far, s_pe, s_cut, s_msgc, s_ed, s_msg, s_hot, s_sum, s_add = (sem(n) for n in ("far_step_dve", "pe_step", "cut_steps", "msg_count_ready", "out_step", "msg_ready", "hot_ready", "sum_psum", "sum_added"))
        s_whot, s_wsum, s_wadd, s_wdve = (sem(n) for n in ("far_hot", "far_sum", "far_added", "far_step"))
        s_aggd, s_ab, s_eb, s_ap, s_al, s_fin, s_out = (sem(n) for n in ("agg_done", "aggb_ready", "out_psum", "alpha_pre", "alpha_ready", "out_ready", "out_written"))

        half = HID
        weight_loads = [(wl[0:MUL, 0:MUL], lin1_ws), (wsc[0:MUL, 0:MUL], sc_ws)]
        for m in range(3):
            weight_loads += [(wl[MUL + m:C:3, MUL + MUL * m:2 * MUL + MUL * m], lin1_wv),
                             (wsc[MUL + m:C:3, MUL + MUL * m:2 * MUL + MUL * m], sc_wv)]
        for t in range(G):
            weight_loads.append((w1[RBF * t:RBF * t + RBF, t // 2, half * (t % 2):half * (t % 2) + half], fc_w1))
        for k in range(2):
            weight_loads += [(w2[half * k:half * k + half, half * k:half * k + half], fc_w2),
                             (w3r[half * k:half * k + half, k, :], fc_w3),
                             (wv2[half * k:half * k + half, :], lin2_wv)]
        weight_loads += [(wagg[0:2 * MUL, 0, 0:MUL], lin2_ws), (wagg[0:2 * MUL, 0, C:C + 1], alpha_w)]
        WZ = 6
        NWL = len(weight_loads)

        block = ctx.enter_context(nc.Block())

        @block.sync
        def _(sp):
            nlast = (NBLK - 1) * P
            for lo, hi in ((0, RA), (RA, ROWS)):
                sp.dma_start(work[lo:hi, W:W + LEN].bitcast(I32), dst.rearrange("(p e) -> p e", p=ROWS)[lo:hi, :]).then_inc(s_dst, 16)
                sp.dma_start(work[lo:hi, 0:LEN], edge_weight.rearrange("(p e) -> p e", p=ROWS)[lo:hi, :]).then_inc(s_dist, 16)
            sp.wait_ge(s_tail, 2)
            sp.dma_start(at_rows[0:NBLK - 1, :], node_vec1[0:nlast, :].rearrange("(b p) c -> b (p c)", p=P)).then_inc(s_at, 16)
            sp.dma_start(at_rows[NBLK - 1:NBLK, 0:TAIL], node_vec1[nlast:N, :].rearrange("(a p) c -> a (p c)", a=1)).then_inc(s_at, 16)
            sp.dma_start(base[:, 0:NBLK - 1, :], x[0:nlast, :].rearrange("(b p) c -> p b c", p=P)).then_inc(s_x, 16)
            sp.dma_start(base[0:TAIL, NBLK - 1, :], x[nlast:N, :]).then_inc(s_x, 16)
            for lo, hi in ((0, RA), (RA, ROWS)):
                sp.dma_start(work[lo:hi, 2 * W:2 * W + LEN].bitcast(I32), src.rearrange("(p e) -> p e", p=ROWS)[lo:hi, :]).then_inc(s_src, 16)
                sp.dma_start(big[lo:hi, (LEN + 1) * REC:(LEN + 1) * REC + 4 * LEN],
                             edge_attr_4.rearrange("(p e) f -> p (e f)", p=ROWS)[lo:hi, :]).then_inc(s_attr, 16)
            sp.wait_ge(s_wz, WZ)
            for n, (to, of) in enumerate(weight_loads):
                sp.dma_start(to, of).then_inc(s_wraw, 16)
            sp.wait_ge(s_recp, 2)
            sp.wait_ge(s_reca, 2)
            sp.wait_ge(s_recd, 1)
            tab = rec_tab[0:E, :].rearrange("(p e) f -> p (e f)", p=ROWS)
            for lo, hi in ((0, RA), (RA, ROWS)):
                sp.dma_start(tab[lo:hi, :], big[lo:hi, 0:LEN * REC]).then_inc(s_rtab, 16)
            sp.dma_start(rec_tab[E:E + 1, :], big[ROWS - 1:ROWS, LEN * REC:(LEN + 1) * REC]).then_inc(s_rtab, 16)
            l1_v = l1_tab.rearrange("(b p) c -> p b c", p=P)
            sp.sem_inc(s_lfree, 1)
            with sp.Fori(0, NI) as i:
                sp.wait_ge(s_lsb, BI * i + BI + 1)
                sp.dma_start(l1_v[:, bass.ds(BI * i, BI), :], lsb[:, :, 0:C]).then_inc(s_ltab, 16)
                sp.wait_ge(s_ltab, 16 * i + 16)
                sp.sem_inc(s_lfree, 1)
            out_v = out[0:nlast, :].rearrange("(b p) c -> p b c", p=P)
            with sp.Fori(0, NI - 1) as i:
                sp.wait_ge(s_fin, i + 1)
                sp.dma_start(out_v[:, bass.ds(BI * i, BI), :], base[:, bass.ds(BI * i, BI), :]).then_inc(s_out, 16)
            sp.wait_ge(s_fin, NI)
            sp.dma_start(out_v[:, BI * (NI - 1):NBLK - 1, :], base[:, BI * (NI - 1):NBLK - 1, :]).then_inc(s_out, 16)
            sp.dma_start(out[nlast:N, :], base[0:TAIL, NBLK - 1, :]).then_inc(s_out, 16)
            sp.wait_ge(s_out, 16 * (NI + 1))

        @block.gpsimd
        def _(po):
            nc.gpsimd.memset(base[:, NBLK - 1, :], 0.0).then_inc(s_tail, 1)
            nc.gpsimd.iota(place1, pattern=[[1, LEN]], base=1, channel_multiplier=0,
                           allow_small_or_imprecise_dtypes=True).then_inc(s_const, 1)
            for m in (wl[:, :], wsc[:, :], w1[:, :, :], w2[:, :], w3r[:, :, :], wagg[:, :, :]):
                nc.gpsimd.memset(m, 0.0).then_inc(s_wz, 1)
            nc.gpsimd.memset(ones[:, :], 1.0).then_inc(s_const, 1)
            nc.gpsimd.memset(half_pi[:, :], pi / 2).then_inc(s_const, 1)
            nc.gpsimd.memset(ident[:, :], 0.0).then_inc(s_pool, 1)
            nc.gpsimd.memset(tri[:, :], 1.0).then_inc(s_pool, 1)
            po.wait_ge(s_pool, 2)
            nc.gpsimd.affine_select(out=ident[:, :], in_=ident[:, :], compare_op=ALU.not_equal, fill=1.0,
                                    base=0, pattern=[[-1, P]], channel_multiplier=1).then_inc(s_const, 1)
            nc.gpsimd.affine_select(out=tri[:, :], in_=tri[:, :], compare_op=ALU.is_gt, fill=0.0,
                                    base=0, pattern=[[1, P]], channel_multiplier=-1).then_inc(s_const, 1)
            nc.gpsimd.iota(iota[:, :], pattern=[[1, WIN]], base=0, channel_multiplier=0,
                           allow_small_or_imprecise_dtypes=True).then_inc(s_const, 1)
            for k in range(RBF):
                nc.gpsimd.memset(kturn[:, k:k + 1], (k + 1) / (2 * CUTOFF)).then_inc(s_const, 1)
                nc.gpsimd.memset(kfreq[:, k:k + 1], (k + 1) * pi / CUTOFF).then_inc(s_const, 1)
            po.wait_ge(s_src, 32)
            nc.gpsimd.tensor_copy(rec_rows[:, 0:LEN, SRC:SRC + 1].rearrange("p e f -> p (e f)"), src_raw.bitcast(I32)).then_inc(s_recp, 1)
            po.wait_ge(s_tno, 1)
            nc.gpsimd.tensor_copy(rec_rows[:, 0:LEN, DST:DST + 1].rearrange("p e f -> p (e f)"), dst_f[:, 0:LEN]).then_inc(s_recp, 1)
            po.wait_ge(s_recp, 1)
            nc.gpsimd.iota(edge_base, pattern=[[1, W]], base=1 - PAD, channel_multiplier=LEN,
                           allow_small_or_imprecise_dtypes=True).then_inc(s_ebase, 1)
            po.wait_ge(s_reca, 1)
            po.wait_ge(s_off, 1)
            nc.gpsimd.iota(tile_no, pattern=[[1, P // 8 + IDW]], base=-(P // 8), channel_multiplier=0,
                           allow_small_or_imprecise_dtypes=True).then_inc(s_ebase, 1)
            po.sem_inc(s_base, 1)
            with po.Fori(0, NI) as i:
                po.wait_ge(s_lsb, BI * i + BI + 1)
                nc.gpsimd.tensor_tensor(base[:, bass.ds(BI * i, BI), :], base[:, bass.ds(BI * i, BI), :],
                                        lsb[:, :, C:2 * C], ALU.add).then_inc(s_base, 1)
            po.wait_ge(s_rtab, 48)
            po.wait_ge(s_ltab, 16 * NI)
            po.wait_ge(s_base, NI + 1)
            nc.gpsimd.memset(big[:, :], 0.0).then_inc(s_agg0, 1)

            def gather_records(s):
                for t in range(G):
                    po.indirect_dma_start(rec[:, s, t, :], None, rec_tab,
                                          bass.IndirectOffsetOnAxis(ids_g[:, s, t:t + 1], 0)).then_inc(s_rec[s], 16)

            def gather_sources(s):
                for t in range(G):
                    po.indirect_dma_start(gath[:, s, t, :], None, l1_tab,
                                          bass.IndirectOffsetOnAxis(src_g[:, s, t:t + 1], 0)).then_inc(s_gat[s], 16)

            po.wait_ge(s_ltab, 16 * NI)
            po.wait_ge(s_nb, 1)
            turns_n = po.value_load(nbody[0:1, 0:1], min_val=1, max_val=NBODY)
            po.wait_ge(s_idg, 1)
            gather_records(0)
            with po.Fori(0, NBODY) as i:
                with po.If(i < turns_n):
                    for s in range(2):
                        g = 2 * i + s
                        po.wait_ge(s_idg, g + 2)
                        po.sem_inc(s_pool)
                        po.wait_ge(s_rc, g + 1)
                        po.sem_inc(s_pool)
                        gather_records(1 - s)
                        po.wait_ge(s_rc, g + 2)
                        po.sem_inc(s_pool)
                        po.wait_ge(s_msg, g + 1)
                        po.sem_inc(s_pool)
                        gather_sources(s)

        @block.scalar
        def _(act):
            act.wait_ge(s_dist, 32)
            nc.scalar.activation(rec_rows[:, 0:LEN, 0:1].rearrange("p e f -> p (e f)"), dist, ACT.Copy).then_inc(s_reca, 1)
            act.wait_ge(s_attr, 32)
            nc.scalar.activation(rec_rows[:, 0:LEN, SH:SH + 4], attr_rows.rearrange("p (e f) -> p e f", f=4), ACT.Copy).then_inc(s_reca, 1)
            act.wait_ge(s_atT, 1)
            nc.scalar.activation(a_in[:, :], ps_a, ACT.Copy, scale=1.0 / sqrt(MUL)).then_inc(s_ain, 1)
            nc.scalar.activation(a_agg[:, :], ps_a, ACT.Copy, scale=1.0 / sqrt(2 * MUL)).then_inc(s_ain, 1)
            act.wait_ge(s_wraw, 16 * NWL)
            nc.scalar.activation(wl[:, C:C + MUL], wsc[:, 0:MUL], ACT.Copy).then_inc(s_wdone, 1)
            nc.scalar.activation(wl[:, C + MUL:2 * C].rearrange("p (o m) -> p m o", m=3),
                                 wsc[:, MUL:C].rearrange("p (m o) -> p m o", m=3), ACT.Copy).then_inc(s_wdone, 1)
            for m in range(3):
                k = m + 1
                rows = slice(HID * (k % 2), HID * (k % 2) + HID)
                nc.scalar.activation(wagg[rows, k // 2, MUL:C].rearrange("p (o m) -> p m o", m=3)[:, m, :],
                                     wv2[rows, :], ACT.Copy).then_inc(s_wdone, 1)
            act.wait_ge(s_var, 1)
            nc.scalar.activation(std[:, :], rstd[:, :], ACT.Sqrt).then_inc(s_std, 1)
            act.wait_ge(s_norm, 1)
            act.wait_ge(s_reca, 2)
            act.wait_ge(s_ain, 2)
            act.sem_inc(s_hT, 1)
            act.sem_inc(s_lsb, 1)
            with act.Fori(0, NI) as i:
                for j in range(BI + 2):
                    if j < BI:
                        b = BI * i + j
                        nc.scalar.activation(hbuf[:, j, :], base[:, bass.ds(b, 1), :].rearrange("p a c -> p (a c)"), ACT.Relu,
                                             scale=rstd[:, bass.ds(b, 1)], bias=nmr[:, bass.ds(b, 1)]).then_inc(s_h, 1)
                    if 1 <= j <= BI:
                        act.wait_ge(s_hTp, BI * i + j)
                        nc.scalar.activation(hT[:, j - 1, :], ps_hT[(j - 1) % 2], ACT.Copy).then_inc(s_hT, 1)
                    if j >= 2:
                        act.wait_ge(s_lp, BI * i + j - 1)
                        if j == 2:
                            act.wait_ge(s_lfree, i + 1)
                            act.wait_ge(s_base, i + 1)
                        nc.scalar.activation(lsb[:, j - 2, :], ps_l[(j - 2) % 4], ACT.Copy,
                                             scale=a_in[:, bass.ds(BI * i + j - 2, 1)]).then_inc(s_lsb, 1)
            act.wait_ge(s_nb, 1)
            turns_n = act.value_load(nbody[0:1, 0:1], min_val=1, max_val=NBODY)
            act.wait_ge(s_ids, 1)

            def edge_numbers(g, s):
                nc.scalar.activation(ids_g[:, s, :], ids[:, bass.ds(G * g, G)], ACT.Copy).then_inc(s_idg, 1)

            def mlp(g):
                act.wait_ge(s_frac, g + 1)
                nc.scalar.activation(sinv[:, :, :], frac[:, :, :], ACT.Sin, scale=2 * pi)
                nc.scalar.activation(cosv[:, :], d6[:, :], ACT.Sin, scale=-pi / (2 * CUTOFF), bias=half_pi[:, 0:1]).then_inc(s_sin, 1)
                act.wait_ge(s_rT, g + 1)
                nc.scalar.activation(rbfT[:, :], ps_z[0:RBF * G, 0:P], ACT.Copy).then_inc(s_rbfT, 1)
                act.wait_ge(s_z1, g + 1)
                nc.scalar.activation(h1[:, :], ps_z, ACT.Silu, scale=1.0 / sqrt(RBF)).then_inc(s_h1, 1)
                act.wait_ge(s_z2, g + 1)
                nc.scalar.activation(h2[:, :], ps_z, ACT.Silu, scale=1.0 / sqrt(HID)).then_inc(s_h2, 1)

            edge_numbers(0, 0)
            edge_numbers(1, 1)
            mlp(0)
            with act.Fori(0, NBODY) as i:
                with act.If(i < turns_n):
                    for s in range(2):
                        g = 2 * i + s + 1
                        act.wait_ge(s_rec[s], P * i + P)
                        edge_numbers(g + 1, s)
                        mlp(g)

            act.wait_ge(s_aggd, 1)

            def sums_out(i, s, first):
                if not first:
                    act.wait_ge(s_eb, i - 1)
                nc.scalar.activation(aggb[s], agg[:, :, bass.ds(BI * P * i, BI * P)], ACT.Copy).then_inc(s_ab, 1)

            def gate(i, s):
                act.wait_ge(s_ap, i + 1)
                nc.scalar.activation(alpha[:, s, :], apre[:, s, :], ACT.Tanh).then_inc(s_al, 1)

            sums_out(0, 0, True)
            sums_out(1, 1, True)
            gate(0, 0)
            sums_out(2, 0, False)
            with act.Fori(0, (NI - 3) // 2) as i:
                for s in range(2):
                    gate(2 * i + 1 + s, 1 - s)
                    sums_out(2 * i + 3 + s, 1 - s, False)
            gate(NI - 2, 1)
            gate(NI - 1, 0)

        @block.vector
        def _(dve):
            v = nc.vector
            step = [0]

            def did(ins):
                step[0] += 1
                ins.then_inc(s_dve, 1)
                return step[0]

            def link(ins):
                dve.wait_ge(s_dve, did(ins))

            v.memset(at_rows[:, :], 0.0).then_inc(s_tail, 1)
            dve.wait_ge(s_dst, 32)
            did(v.tensor_copy(dst_f[:, 0:LEN], dst_raw.bitcast(I32)))
            did(v.memset(dst_f[:, LEN:LEN + 1], -1.0))
            did(v.memset(last1[:, 0:1], 0.0))
            dve.wait_ge(s_dve, 3)
            v.tensor_tensor(listed, dst_f[:, 0:LEN], dst_f[:, 1:LEN + 1], ALU.not_equal).then_inc(s_tno, 1)
            dve.wait_ge(s_dist, 32)
            dve.wait_ge(s_tno, 1)
            link(v.scalar_tensor_tensor(out=listed, in0=dist, scalar=CUTOFF, in1=listed, op0=ALU.is_le, op1=ALU.max))
            did(v.tensor_tensor_scan(out=rank, data0=listed, data1=listed, initial=0.0, op0=ALU.add, op1=ALU.max))
            dve.wait_ge(s_const, 1)
            link(v.tensor_tensor(mark1, listed, place1, ALU.mult))
            v.tensor_copy(tile0_f[:, :], rank[:, LEN - 1:LEN]).then_inc(s_cnt, 1)
            link(v.tensor_tensor_scan(out=last1[:, 1:LEN + 1], data0=mark1, data1=mark1, initial=0.0, op0=ALU.max, op1=ALU.max))
            did(v.tensor_tensor(rec_rows[:, 0:LEN, CNT:CNT + 1].rearrange("p e f -> p (e f)"), place1, last1[:, 0:LEN], ALU.subtract))
            link(v.memset(rec_rows[:, LEN, :], 0.0))
            did(v.memset(rec_rows[:, LEN, 0:1], 8 * CUTOFF))
            v.tensor_copy(rec_rows[:, LEN, DST:DST + 1], dst_f[:, LEN - 1:LEN]).then_inc(s_recd, 1)

            dve.wait_ge(s_x, 32)
            k0, LNS = step[0], 2 * BI + 1
            with dve.Fori(0, NI) as i:
                for j in range(BI):
                    if j == 0:
                        dve.wait_ge(s_dve, LNS * i + k0)
                    v.bn_stats(stats[:, j, :], base[:, bass.ds(BI * i + j, 1), :].rearrange("p a c -> p (a c)")).then_inc(s_dve, 1)
                dve.wait_ge(s_dve, LNS * i + k0 + BI)
                dve.sem_inc(s_ln, 1)
                for j in range(BI):
                    v.bn_aggr(mv7[:, j, :], stats[:, j, :]).then_inc(s_dve, 1)
                dve.wait_ge(s_dve, LNS * i + k0 + 2 * BI)
                v.tensor_copy(mv[:, bass.ds(BI * i, BI), :], mv7[:, :, :]).then_inc(s_dve, 1)
            step[0] += LNS * NI
            dve.wait_ge(s_dve, step[0])
            v.tensor_scalar(rstd[:, :], mv[:, :, 1], EPS, None, ALU.add).then_inc(s_var, 1)
            dve.wait_ge(s_std, 1)
            link(v.reciprocal(rstd[:, :], std[:, :]))
            v.scalar_tensor_tensor(out=nmr[:, :], in0=mv[:, :, 0], scalar=-1.0, in1=rstd[:, :], op0=ALU.mult, op1=ALU.mult).then_inc(s_norm, 1)

            dve.wait_ge(s_pre, 1)
            link(v.tensor_copy(base_i[:, :], ps_start))
            did(v.tensor_single_scalar(tile0_i[:, :], base_i[:, :], 7, ALU.logical_shift_right))
            did(v.tensor_single_scalar(off_i[:, :], base_i[:, :], P - 1, ALU.bitwise_and))
            link(v.tensor_scalar(tot_i[:, :], ps_total, float(BODY * P - 1), None, ALU.add))
            did(v.tensor_copy(tile0_f[:, :], tile0_i[:, :]))
            link(v.tensor_copy(off_f[:, :], off_i[:, :]))
            v.tensor_single_scalar(nbody[:, :], tot_i[:, :], 11, ALU.logical_shift_right).then_inc(s_nb, 1)
            did(v.tensor_scalar(pad_off[:, :], off_f[:, :], -1.0, float(PAD), ALU.mult, ALU.add))
            link(v.tensor_tensor(shift0, place1, rank, ALU.subtract))
            did(v.memset(sh_a[:, 0:PAD], 0))
            did(v.memset(sh_a[:, PAD + LEN:W], 0))
            did(v.memset(move, 0))
            dve.wait_ge(s_dve, step[0])
            v.scalar_tensor_tensor(out=sh_a[:, PAD:PAD + LEN], in0=shift0, scalar=pad_off[:, 0:1], in1=listed,
                                   op0=ALU.add, op1=ALU.mult).then_inc(s_off, 1)
            dve.wait_ge(s_off, 1)

            now, new = sh_a, sh_b
            for k in range(STEPS):
                link(v.tensor_scalar(stay, now, k, 1, ALU.logical_shift_right, ALU.bitwise_and))
                link(v.tensor_tensor(move[:, 0:W], stay, now, ALU.mult))
                link(v.tensor_tensor(stay, now, move[:, 0:W], ALU.subtract))
                link(v.tensor_tensor(new, stay, move[:, 2 ** k:2 ** k + W], ALU.add))
                now, new = new, now

            dve.wait_ge(s_ebase, 2)
            dve.wait_ge(s_recp, 2)
            n = did(v.scalar_tensor_tensor(out=edge_no, in0=now, scalar=0.0, in1=edge_base, op0=ALU.is_gt, op1=ALU.mult))
            link(v.tensor_scalar(tile_hot, tile_no, tile0_f[:, 0:1], None, ALU.is_equal))
            v.tensor_tensor(edge_no, edge_no, now, ALU.add).then_inc(s_hotid, 1)
            dve.wait_ge(s_wraw, 16 * NWL)
            did(v.tensor_scalar(w3[:, :, 0:3 * MUL], w3r[:, :, 0:3 * MUL], 1.0 / sqrt(HID), None, ALU.mult))
            did(v.tensor_scalar(w3[:, :, 3 * MUL:C], w3r[:, :, 3 * MUL:C], 1.0 / sqrt(HID) / sqrt(3.0), None, ALU.mult))
            dve.wait_ge(s_nb, 1)
            turns_n = dve.value_load(nbody[0:1, 0:1], min_val=1, max_val=NBODY)

            def ids_out(c):
                dve.wait_ge(s_idp, c + 1)
                link(v.tensor_scalar(none[:, :], ps_id, 0.0, float(E + 1), ALU.is_equal, ALU.mult))
                v.scalar_tensor_tensor(out=ids[:, IDC * c:IDC * (c + 1)], in0=ps_id, scalar=-1.0, in1=none[:, :],
                                       op0=ALU.add, op1=ALU.add).then_inc(s_ide, 1)
                dve.wait_ge(s_ide, c + 1)

            ids_out(0)
            for c in range(1, NIDC):
                with dve.If(turns_n > IDC // BODY * c - 1):
                    dve.wait_ge(s_idp, c + 1)
                    v.tensor_scalar(none[:, :], ps_id, 0.0, float(E + 1), ALU.is_equal, ALU.mult).then_inc(s_ide2, 1)
                    dve.wait_ge(s_ide2, c)
                    v.scalar_tensor_tensor(out=ids[:, IDC * c:IDC * (c + 1)], in0=ps_id, scalar=-1.0, in1=none[:, :],
                                           op0=ALU.add, op1=ALU.add).then_inc(s_ide, 1)
                    dve.wait_ge(s_ide, c + 1)
            v.memset(msg[:, :, 2 * C:MSG], 0.0).then_inc(s_ids, 1)
            dve.wait_ge(s_ids, 1)

            sh = [recw[:, s, :, SH:SH + 4] for s in range(2)]
            K1, K2, K3 = 12, 5, 8
            L1 = step[0]
            PER = K1 + K2 + K3

            class Steps:
                def __init__(self, start):
                    self.start, self.n = start, 0

                def did(self, ins):
                    self.n += 1
                    ins.then_inc(s_dve, 1)
                    return self.n

                def need(self, n):
                    dve.wait_ge(s_dve, self.start + n)

            def radial(g, s, i, own, first=False):
                dve.wait_ge(s_rec[s], P * i + P)
                own.did(v.tensor_copy(recw[:, s, :, :], rec[:, s, :, :]))
                a = own.did(v.tensor_scalar(d6[:, :], rec[:, s, :, 0], CUTOFF, None, ALU.min))
                v.tensor_copy(src_g[:, s, :], rec[:, s, :, SRC]).then_inc(s_rc, 1)
                own.need(a)
                dm = d6[:, :].unsqueeze(2).broadcast_to([P, G, RBF])
                a = own.did(v.tensor_tensor(turns[:, :, :], dm, kturn[:, :].unsqueeze(1).broadcast_to([P, G, RBF]), ALU.mult))
                b = own.did(v.tensor_tensor(fd[:, :, :], dm, kfreq[:, :].unsqueeze(1).broadcast_to([P, G, RBF]), ALU.mult))
                own.need(a)
                a = own.did(v.tensor_scalar(whole[:, :, :], turns[:, :, :], ROUND, ROUND, ALU.add, ALU.subtract))
                own.need(b)
                b = own.did(v.scalar_tensor_tensor(out=rfd[:, :, :], in0=fd[:, :, :], scalar=-1.0, in1=fd[:, :, :], op0=ALU.mult, op1=ALU.max))
                own.need(b)
                own.did(v.tensor_scalar(small[:, :, :], rfd[:, :, :], SMALL, None, ALU.is_lt))
                own.need(own.n)
                v.tensor_tensor(frac[:, :, :], turns[:, :, :], whole[:, :, :], ALU.subtract).then_inc(s_frac, 1)
                one64 = ones[:, 0:G * RBF].rearrange("p (t k) -> p t k", t=G)
                a = own.did(v.copy_predicated(fd[:, :, :], small[:, :, :], one64))
                if not first:
                    dve.wait_ge(s_rT, g)
                own.did(v.tensor_copy(dst_c[:, :], recw[:, s, :, DST]))
                own.need(a)
                a = own.did(v.reciprocal(rfd[:, :, :], fd[:, :, :]))
                dve.wait_ge(s_sin, g + 1)
                own.need(a)
                a = own.did(v.tensor_tensor(cut2[:, :], cosv[:, :], cosv[:, :], ALU.mult))
                b = own.did(v.tensor_tensor(rb[:, :, :], sinv[:, :, :], rfd[:, :, :], ALU.mult))
                own.need(b)
                v.scalar_tensor_tensor(out=cut[:, :], in0=recw[:, s, :, 0], scalar=CUTOFF, in1=cut2[:, :],
                                       op0=ALU.is_le, op1=ALU.mult).then_inc(s_cut, 1)
                v.copy_predicated(rb[:, :, :], small[:, :, :], one64).then_inc(s_cut, 1)
                dve.wait_ge(s_cut, 2 * g + 2)
                v.tensor_tensor(rbf[:, :].rearrange("p (t k) -> p t k", t=G), rb[:, :, :],
                                cut[:, :].unsqueeze(2).broadcast_to([P, G, RBF]), ALU.mult).then_inc(s_rbf, 1)
                assert own.n == K1, own.n

            def extent(g, own):
                dve.wait_ge(s_rT, g + 1)
                own.did(v.tensor_reduce(minmax[:, 0:1], ps_x[0:G, P:2 * P], AX_X, ALU.min))
                a = own.did(v.tensor_reduce(minmax[:, 1:2], ps_x[0:G, P:2 * P], AX_X, ALU.max))
                own.need(a)
                v.tensor_tensor(diag[:, :, :], ident[0:G, 0:G].unsqueeze(1).broadcast_to([G, 2, G]),
                                minmax[:, :].unsqueeze(2).broadcast_to([G, 2, G]), ALU.mult).then_inc(s_diag, 1)

            def windows(g, s, own):
                dve.wait_ge(s_bc, g + 1)
                lows = ps_x[:, 2 * P:2 * P + G].rearrange("p (q t) -> p q t", t=2)
                highs = ps_x[:, 2 * P + G:2 * P + 2 * G].rearrange("p (q t) -> p q t", t=2)
                own.did(v.tensor_reduce(win0[:, :], lows, AX_X, ALU.min))
                a = own.did(v.tensor_reduce(winmax[:, :], highs, AX_X, ALU.max))
                own.need(a)
                a = own.did(v.tensor_tensor(span4[:, :], winmax[:, :], win0[:, :], ALU.subtract))
                v.tensor_copy(win0_i[:, :], win0[:, :]).then_inc(s_win, 1)
                v.tensor_tensor(dloc[:, :].rearrange("p (q t) -> p q t", t=2),
                                recw[:, s, :, DST].rearrange("p (q t) -> p q t", t=2),
                                win0[:, :].unsqueeze(2).broadcast_to([P, NPAIR, 2]), ALU.subtract).then_inc(s_win, 1)
                own.need(a)
                v.tensor_reduce(span_i[:, :], span4[:, :], AX_X, ALU.max).then_inc(s_win, 1)

            def messages(g, s, i, own):
                gs, gv = gath[:, s, :, 0:MUL], gath[:, s, :, MUL:C].rearrange("p t (m c) -> p t m c", m=3)
                w = ps_w[s]
                shm = sh[s][:, :, 1:4].unsqueeze(3).broadcast_to([P, G, 3, MUL])
                dve.wait_ge(s_gat[s], P * i + P)
                ga = own.did(v.tensor_tensor(gsh0[:, :, :], gath[:, s, :, :], sh[s][:, :, 0:1].broadcast_to([P, G, C]), ALU.mult))
                tv = own.did(v.tensor_tensor(gsh1[:, :, :, :], gv, shm, ALU.mult))
                dve.wait_ge(s_w, g + 1)
                tt = own.did(v.tensor_tensor(t01[:, :, :], gs, w[:, :, MUL:2 * MUL], ALU.mult))
                own.need(tv)
                d1 = own.did(v.tensor_tensor(dot1[:, :, :], gsh1[:, :, 0, :], gsh1[:, :, 1, :], ALU.add))
                own.did(v.tensor_tensor(msg[:, :, 0:MUL], gsh0[:, :, 0:MUL], w[:, :, 0:MUL], ALU.mult))
                own.need(d1)
                d2 = own.did(v.tensor_tensor(dot2[:, :, :], dot1[:, :, :], gsh1[:, :, 2, :], ALU.add))
                mv_ = msg[:, :, 2 * MUL:2 * C].rearrange("p t (m k c) -> p t m k c", m=3, k=2)
                own.did(v.tensor_tensor(mv_[:, :, :, 1, :], gsh0[:, :, MUL:C].rearrange("p t (m c) -> p t m c", m=3),
                                        w[:, :, 2 * MUL:3 * MUL].unsqueeze(2).broadcast_to([P, G, 3, MUL]), ALU.mult))
                own.need(d2)
                own.did(v.tensor_tensor(msg[:, :, MUL:2 * MUL], dot2[:, :, :], w[:, :, 3 * MUL:C], ALU.mult))
                v.tensor_tensor(mv_[:, :, :, 0, :], t01[:, :, :].unsqueeze(2).broadcast_to([P, G, 3, MUL]), shm, ALU.mult).then_inc(s_msg, 1)
                v.tensor_copy(msg[:, :, 2 * C:2 * C + 1], recw[:, s, :, CNT:CNT + 1]).then_inc(s_msgc, 1)

            def one_hot(to):
                return v.tensor_tensor(to, iota[:, :].unsqueeze(1).broadcast_to([P, G, WIN]),
                                       dloc[:, :].unsqueeze(2).broadcast_to([P, G, WIN]), ALU.is_equal)

            def add_window(q, start):
                part = agg[:, :, bass.ds(start, WIN)]
                return v.tensor_tensor(part, part, ps_s[q % 2], ALU.add)

            far_turns = dve.alloc_register("far_turns_dve")
            dve.reg_mov(far_turns, 0)

            def far_windows(g):
                first = dve.snap(far_turns)
                dve.wait_ge(s_add, NPAIR * g + NPAIR + 2)
                dve.sem_inc(s_far, 1)
                with dve.Fori(0, NBLK - 1) as k:
                    turn = first + k
                    dve.wait_ge(s_whot, turn + 1)
                    v.tensor_scalar(dloc[:, :], dloc[:, :], float(WIN), None, ALU.subtract).then_inc(s_wdve, 1)
                    v.tensor_scalar(win0_i[:, :], win0_i[:, :], WIN, NBLK * P, ALU.add, ALU.min).then_inc(s_wdve, 1)
                    dve.wait_ge(s_wdve, 2 * turn + 2)
                    one_hot(hot[:, :, :]).then_inc(s_whot, 1)
                    for q in range(NPAIR):
                        start = dve.value_load(win0_i[0:1, q:q + 1], min_val=0, max_val=NBLK * P)
                        dve.wait_ge(s_wsum, NPAIR * turn + q + 1)
                        dve.wait_ge(s_wadd, NPAIR * turn + q + 1)
                        add_window(q, start).then_inc(s_wadd, 1)
                dve.wait_ge(s_wadd, NPAIR * first + (NPAIR * (NBLK - 1) + 1))
                dve.sem_inc(s_far, 1)
                dve.reg_add(far_turns, far_turns, NBLK - 1)
            own = Steps(L1)
            dve.sem_inc(s_rc, 1)
            dve.sem_inc(s_msg, 2)
            dve.wait_ge(s_agg0, 1)
            dve.sem_inc(s_add, 2)
            dve.sem_inc(s_whot, 1)
            dve.sem_inc(s_wadd, 1)
            radial(0, 0, 0, own, first=True)
            extent(0, own)
            windows(0, 0, own)
            start0 = L1 + own.n
            with dve.Fori(0, NBODY) as i:
                with dve.If(i < turns_n):
                    own = Steps(i * (2 * PER) + start0)
                    for s in range(2):
                        g = 2 * i + s
                        own.n = 0
                        own.start = i * (2 * PER) + (start0 + s * PER)
                        radial(g + 1, 1 - s, i + s, own)
                        messages(g, s, i, own)
                        extent(g + 1, own)
                        dve.wait_ge(s_win, 3 * g + 3)
                        one_hot(hot[:, :, :]).then_inc(s_hot, 1)
                        for q in range(NPAIR):
                            start = dve.value_load(win0_i[0:1, q:q + 1], min_val=0, max_val=N - 1)
                            dve.wait_ge(s_sum, NPAIR * g + q + 1)
                            dve.wait_ge(s_add, NPAIR * g + q + 2)
                            add_window(q, start).then_inc(s_add, 1)
                        span = dve.value_load(span_i[0:1, 0:1], min_val=0, max_val=N)
                        with dve.If(span >= WIN):
                            far_windows(g)
                        windows(g + 1, 1 - s, own)
                        assert own.n == PER, own.n
            dve.wait_ge(s_add, 2 * NPAIR * turns_n + 2)
            dve.sem_inc(s_aggd, 1)

            def finish(i, s):
                own_e = EP * i
                dve.wait_ge(s_eb, i + 1)
                v.tensor_scalar(cmax[:, s, :], ps_c[s], 1.0, None, ALU.max).then_inc(s_ed, 1)
                dve.wait_ge(s_ed, own_e + 1)
                v.reciprocal(rcnt[:, s, :], cmax[:, s, :]).then_inc(s_ed, 1)
                dve.wait_ge(s_ed, own_e + 2)
                v.tensor_tensor(scale[:, s, :], rcnt[:, s, :], a_agg[:, bass.ds(BI * i, BI)], ALU.mult).then_inc(s_ed, 1)
                dve.wait_ge(s_ed, own_e + 3)
                for k in range(3):
                    nb = min(3, BI - 3 * k)
                    v.tensor_tensor(apre[:, s, 3 * k:3 * k + nb],
                                    ps[:, 3 * s + k, 0:3 * (C + 1)].rearrange("p (b c) -> p b c", c=C + 1)[:, 0:nb, C],
                                    scale[:, s, 3 * k:3 * k + nb], ALU.mult).then_inc(s_ap if k == 2 else s_ed, 1)
                dve.wait_ge(s_al, i + 1)
                v.tensor_tensor(salpha[:, s, :], alpha[:, s, :], scale[:, s, :], ALU.mult).then_inc(s_ed, 1)
                dve.wait_ge(s_ed, own_e + 6)
                for j in range(BI):
                    to = base[:, bass.ds(BI * i + j, 1), :].rearrange("p a c -> p (a c)")
                    ins = v.scalar_tensor_tensor(out=to, in0=ps_e(s, j)[:, 0:C], scalar=salpha[:, s, j:j + 1], in1=to,
                                                 op0=ALU.mult, op1=ALU.add)
                ins.then_inc(s_fin, 1)

            EP = 6
            dve.wait_ge(s_base, NI + 1)
            with dve.Fori(0, (NI - 1) // 2) as i:
                finish(2 * i, 0)
                finish(2 * i + 1, 1)
            finish(NI - 1, 0)

        @block.tensor
        def _(pe):
            mm = nc.tensor.matmul
            NCONST = 6 + 2 * RBF
            pe.wait_ge(s_const, NCONST)
            pe.wait_ge(s_at, 32)
            nc.tensor.transpose(ps_a, at_rows[:, :], ident[0:NBLK, 0:NBLK]).then_inc(s_atT, 1)
            pe.wait_ge(s_cnt, 1)
            mm(ps_start, tri[0:ROWS, 0:ROWS], tile0_f[:, :], start=True, stop=True)
            mm(ps_total, ones[0:ROWS, :], tile0_f[:, :], start=True, stop=True).then_inc(s_pre, 1)
            pe.wait_ge(s_wdone, 5)
            with pe.Fori(0, NI) as i:
                for j in range(BI + 1):
                    if j < BI:
                        pe.wait_ge(s_h, BI * i + j + 1)
                        pe.wait_ge(s_hT, BI * i + max(j, 1))
                        nc.tensor.transpose(ps_hT[j % 2], hbuf[:, j, :], ident[:, :]).then_inc(s_hTp, 1)
                    if j >= 1:
                        pe.wait_ge(s_hT, BI * i + j + 1)
                        pe.wait_ge(s_lsb, BI * i + max(j - 4, 0) + 1)
                        mm(ps_l[(j - 1) % 4], hT[:, j - 1, :], wl[:, :], start=True, stop=True).then_inc(s_lp, 1)
            pe.wait_ge(s_hotid, 1)

            def ids_of(c):
                for k in range(LCH):
                    at = P // 8 - k + IDC * c
                    last = mm(ps_id, edge_no[:, P * k:P * (k + 1)], tile_hot[:, at:at + IDC], start=(k == 0), stop=(k == LCH - 1))
                last.then_inc(s_idp, 1)

            ids_of(0)
            pe.wait_ge(s_nb, 1)
            turns_n = pe.value_load(nbody[0:1, 0:1], min_val=1, max_val=NBODY)
            for c in range(1, NIDC):
                with pe.If(turns_n > IDC // BODY * c - 1):
                    pe.wait_ge(s_ide, c)
                    ids_of(c)
            pe.wait_ge(s_ids, 1)
            pe.wait_ge(s_lsb, NBLK + 1)

            def radial_mlp(g, s, first):
                pe.wait_ge(s_rbf, g + 1)
                nc.tensor.transpose(ps_x[0:G, P:2 * P], dst_c[:, :], ident[:, :])
                nc.tensor.transpose(ps_z[0:RBF * G, 0:P], rbf[:, :], ident[:, :]).then_inc(s_rT, 1)
                pe.wait_ge(s_rbfT, g + 1)
                for j in range(4):
                    last = mm(ps_z[:, P * j:P * (j + 1)], w1[:, j, :], rbfT[:, :], start=True, stop=True)
                last.then_inc(s_z1, 1)
                pe.wait_ge(s_h1, g + 1)
                mm(ps_z, w2[:, :], h1[:, :], start=True, stop=True).then_inc(s_z2, 1)
                pe.wait_ge(s_h2, g + 1)
                if not first:
                    pe.wait_ge(s_msg, g + 1)
                for j in range(4):
                    last = mm(ps_w[s][:, 2 * j:2 * j + 2, :], h2[:, P * j:P * (j + 1)], w3[:, :, :], start=True, stop=True)
                last.then_inc(s_w, 1)

            def spread(g):
                pe.wait_ge(s_diag, g + 1)
                mm(ps_x[:, 2 * P:2 * P + 2 * G], ones[0:G, :], diag[:, :, :], start=True, stop=True).then_inc(s_bc, 1)

            def pair_sum(q):
                for c in range(FC):
                    for t in range(2):
                        last = mm(ps_s[q % 2][:, c, :], msg[:, 2 * q + t, P * c:P * (c + 1)], hot[:, 2 * q + t, :],
                                  start=(t == 0), stop=(t == 1))
                return last

            far_turns = pe.alloc_register("far_turns_pe")
            pe.reg_mov(far_turns, 0)

            def far_windows():
                first = pe.snap(far_turns)
                with pe.Fori(0, NBLK - 1) as k:
                    turn = first + k
                    pe.wait_ge(s_whot, turn + 2)
                    for q in range(NPAIR):
                        if q >= 2:
                            pe.wait_ge(s_wadd, NPAIR * turn + q)
                        pair_sum(q).then_inc(s_wsum, 1)
                pe.reg_add(far_turns, far_turns, NBLK - 1)

            radial_mlp(0, 0, True)
            spread(0)
            with pe.Fori(0, NBODY) as i:
                with pe.If(i < turns_n):
                    for s in range(2):
                        g = 2 * i + s
                        radial_mlp(g + 1, 1 - s, False)
                        spread(g + 1)
                        pe.wait_ge(s_hot, g + 1)
                        pe.sem_inc(s_pe, 1)
                        span = pe.value_load(span_i[0:1, 0:1], min_val=0, max_val=N)
                        for q in range(NPAIR):
                            pe.wait_ge(s_add, NPAIR * g + q + 1)
                            pair_sum(q).then_inc(s_sum, 1)
                        with pe.If(span >= WIN):
                            far_windows()
                        pe.sem_inc(s_pe, 1)

            def project(i, s, free):
                pe.wait_ge(s_ab, i + 1)
                if free is not None:
                    pe.wait_ge(s_fin, free)
                for j in range(BI):
                    nodes = slice(P * j, P * (j + 1))
                    mm(ps_c[s][:, j:j + 1], aggb[s][0:1, 2, nodes], ones[0:1, 0:1], start=True, stop=True)
                    for c in range(2):
                        last = mm(ps_e(s, j), aggb[s][:, c, nodes], wagg[:, c, :], start=(c == 0), stop=(c == 1))
                last.then_inc(s_eb, 1)

            project(0, 0, None)
            project(1, 1, None)
            with pe.Fori(0, (NI - 3) // 2) as i:
                project(2 * i + 2, 0, 2 * i + 1)
                project(2 * i + 3, 1, 2 * i + 2)
            project(NI - 1, 0, NI - 2)


_INS = ['x', 'src', 'dst', 'edge_attr_4', 'edge_weight', 'node_vec1', 'L0_gnn_sc_ws', 'L0_gnn_sc_wv', 'L0_gnn_lin1_ws',
        'L0_gnn_lin1_wv', 'L0_gnn_fc_w1', 'L0_gnn_fc_w2', 'L0_gnn_fc_w3', 'L0_gnn_lin2_ws', 'L0_gnn_lin2_wv', 'L0_gnn_alpha_w']


def kernel(**inputs):
    import concourse.bacc as bacc
    from concourse.bass_utils import run_bass_kernel_spmd

    nc = bacc.Bacc("TRN2", target_bir_lowering=False, num_devices=1)
    arrays, args = {}, []
    for name in _INS:
        a = np.ascontiguousarray(inputs[name])
        arrays[f"in_{name}"] = a
        args.append(nc.dram_tensor(f"in_{name}", a.shape, mybir.dt.from_np(a.dtype), kind="ExternalInput").ap())
    args.append(nc.dram_tensor("out_x", (N, C), F32, kind="ExternalOutput").ap())
    gnn_kernel(nc, *args)
    r = run_bass_kernel_spmd(nc, [arrays], core_ids=[0])
    return r.results[0]["out_x"]
```

```python
from contextlib import ExitStack
from math import pi, sqrt

import numpy as np
import concourse.bass as bass
from concourse import mybir

F32 = mybir.dt.float32
I32 = mybir.dt.int32
I16 = mybir.dt.int16
BF16 = mybir.dt.bfloat16
ALU = mybir.AluOpType
ACT = mybir.ActivationFunctionType
AX_X = mybir.AxisListType.X

P = 128
N = 6250
C = 128
E = 200000
MUL = 32
RBF = 8
HID = 64
CUTOFF = 6.0
SMALL = 1e-6
EPS = 1e-5
ROUND = 1.5 * 2.0 ** 23

NBLK = -(-N // P)
BI = 7
NI = NBLK // BI
TAIL = N - (NBLK - 1) * P

ROWS = 125
LEN = E // ROWS
RA = 112
PAD = P
W = 14 * P
CW = W + 32
STEPS = 11
LCH = W // P

G = 8
NPAIR = G // 2
GIN = 16 * G
TILES = -(-E // P)
BODY = 2 * G
NBODY = -(-TILES // BODY)
TURNS_IN = 7
TURNS_OUT = NBODY // TURNS_IN
IDC = 2 * P
NIDC = -(-(NBODY * BODY + 4 * G) // IDC)
IDW = IDC * NIDC
REC = 8
SRC, DST, CNT, SH = 1, 2, 3, 4

FC = 3
WIN = 160
AGGW = NBLK * P + WIN + 8
FAR = -(-N // WIN)


def gnn_kernel(nc, x, src, dst, edge_attr_4, edge_weight, node_vec1, sc_ws, sc_wv, lin1_ws, lin1_wv,
               fc_w1, fc_w2, fc_w3, lin2_ws, lin2_wv, alpha_w, out):
    rec_tab = nc.dram_tensor("rec_tab", (E + 1, REC), F32, kind="Internal").ap()
    l1_tab = nc.dram_tensor("l1_tab", (NBLK * P, C), F32, kind="Internal").ap()

    ctx = ExitStack()
    with ctx:
        def sb(name, shape, dt=F32):
            return ctx.enter_context(nc.sbuf_tensor(name, shape, dt))

        def sem(name):
            return ctx.enter_context(nc.semaphore(name))

        big = sb("big", [P, FC * AGGW])
        rec_rows = big[0:ROWS, 0:(LEN + 1) * REC].rearrange("p (e f) -> p e f", f=REC)
        attr_rows = big[0:ROWS, (LEN + 1) * REC:(LEN + 1) * REC + 4 * LEN]
        at_h = (LEN + 1) * REC
        hbuf = big[:, at_h:at_h + BI * C].rearrange("p (b c) -> p b c", b=BI)
        hT = big[:, at_h + BI * C:at_h + 2 * BI * C].rearrange("p (b c) -> p b c", b=BI)
        lsb = big[:, at_h + 2 * BI * C:at_h + 6 * BI * C].rearrange("p (b c) -> p b c", b=2 * BI)
        agg = big[:, :].rearrange("p (c n) -> p c n", c=FC)

        work = sb("work", [P, 8 * CW + 3 * W // 2 + (W + 1024) // 2])

        def col(n, width=W):
            return work[0:ROWS, n * CW:n * CW + width]

        dist, dst_raw, src_raw, dst_f = col(0, LEN), col(1, LEN), col(2, LEN), col(3, LEN + 1)
        place1, rank, run_start, listed = col(4, LEN), col(5, LEN), col(6, LEN + 1), col(7, LEN + 1)
        near, tile_no = col(0, LEN), col(0, P // 8 + IDW)
        end_mark, shift0, tile_hot = col(1, LEN), col(1, LEN), col(1, P // 8 + IDW)
        edge_base, edge_no = col(2), col(3)
        near_last, run_end = col(5, LEN), col(0, LEN)
        at16 = 8 * CW
        sh_a = work[0:ROWS, at16:at16 + W // 2].bitcast(I16)
        sh_b = work[0:ROWS, at16 + W // 2:at16 + W].bitcast(I16)
        temp = work[0:ROWS, at16:at16 + LEN + 1]
        stay = work[0:ROWS, at16 + W:at16 + 3 * W // 2].bitcast(I16)
        move = work[0:ROWS, at16 + 3 * W // 2:at16 + 3 * W // 2 + (W + 1024) // 2].bitcast(I16)

        used = [0]

        def carve(*shape):
            n = int(np.prod(shape))
            v = work[:, used[0]:used[0] + n]
            used[0] += n
            if len(shape) == 2:
                return v.rearrange("p (a b) -> p a b", a=shape[0])
            if len(shape) == 3:
                return v.rearrange("p (a b c) -> p a b c", a=shape[0], b=shape[1])
            return v

        gath = carve(2, G, C)
        gsh0 = carve(G, C)
        gsh1 = carve(G, 3, MUL)
        t01 = carve(G, MUL)
        dot1, dot2 = carve(G, MUL), carve(G, MUL)
        msg = carve(G, 2 * C)
        hot = carve(2, G, WIN)
        hot16 = carve(G * WIN // 2).bitcast(BF16).rearrange("p (t n) -> p t n", t=G)
        aggb = [carve(2, BI * P), carve(2, BI * P)]
        assert used[0] <= 8 * CW + 3 * W // 2 + (W + 1024) // 2, used[0]

        base = sb("base", [P, NBLK, C])
        ids = sb("ids", [P, IDW], I32)
        rec, recw = sb("rec", [P, 2, G, REC]), sb("recw", [P, 2, G, REC])
        ids_g, src_g = sb("ids_g", [P, 2, G], I32), sb("src_g", [P, 2, G], I32)
        rbfT, h1, h2 = sb("rbfT", [RBF * G, P]), sb("h1", [P, 4 * P]), sb("h2", [P, 4 * P])
        d6, cosv, cut2, cut = sb("d6", [P, G]), sb("cosv", [P, G]), sb("cut2", [P, G]), sb("cut", [P, G])
        turns, whole, frac = sb("turns", [P, G, RBF]), sb("whole", [P, G, RBF]), sb("frac", [P, G, RBF])
        fd, rfd, sinv = sb("fd", [P, G, RBF]), sb("rfd", [P, G, RBF]), sb("sinv", [P, G, RBF])
        small = sb("small", [P, G, RBF], I32)
        rb, rbf = sb("rb", [P, G, RBF]), sb("rbf", [P, G * RBF])
        dst_c = sb("dst_c", [P, G])
        minmax, diag = sb("minmax", [G, 2]), sb("diag", [G, 2, G])
        win0, winmax, span4 = sb("win0", [P, NPAIR]), sb("winmax", [P, NPAIR]), sb("span4", [P, NPAIR])
        win0_i, span_i = sb("win0_i", [P, 2, NPAIR], I32), sb("span_i", [P, 2], I32)
        dloc = sb("dloc", [P, 2, G])
        cnt16 = sb("cnt16", [P, G, P], BF16)

        ident, iota, tri = sb("ident", [P, P]), sb("iota", [P, WIN]), sb("tri", [P, P])
        ones, half_pi = sb("ones", [P, P]), sb("half_pi", [P, 1])
        kturn, kfreq = sb("kturn", [P, RBF]), sb("kfreq", [P, RBF])
        w1, w2 = sb("w1", [RBF * G, 4, P]), sb("w2", [P, P])
        w3r, w3 = sb("w3r", [P, 2, C]), sb("w3", [P, 2, C])
        wl = sb("wl", [P, 2 * C])
        wsc = sb("wsc", [P, C])
        wagg, wv2 = sb("wagg", [P, 2, C + 1]), sb("wv2", [P, MUL])
        at_rows, cnt_rows = sb("at_rows", [NBLK, P]), sb("cnt_rows", [NBLK, 2, P])
        a_norm, a_in, a_agg = sb("a_norm", [P, NBLK]), sb("a_in", [P, NBLK]), sb("a_agg", [P, NBLK])
        stats, mv7, mv = sb("stats", [P, BI, 6]), sb("mv7", [P, BI, 2]), sb("mv", [P, NBLK, 2])
        std, rstd, nmean = sb("std", [P, NBLK]), sb("rstd", [P, NBLK]), sb("nmean", [P, NBLK])
        base_i, tile0_i, off_i = sb("base_i", [ROWS, 1], I32), sb("tile0_i", [ROWS, 1], I32), sb("off_i", [ROWS, 1], I32)
        tile0_f, off_f, pad_off = sb("tile0_f", [ROWS, 1]), sb("off_f", [ROWS, 1]), sb("pad_off", [ROWS, 1])
        tot_i, nbody = sb("tot_i", [P, 1], I32), sb("nbody", [P, 1], I32)
        none = sb("none", [P, IDC])
        cnt_n, cmax, rcnt, scale = (sb(n, [P, NBLK]) for n in ("cnt_n", "cmax", "rcnt", "scale"))
        apre, alpha, salpha = sb("apre", [P, 2, BI]), sb("alpha", [P, 2, BI]), sb("salpha", [P, 2, BI])

        ps = ctx.enter_context(nc.psum_tensor("ps", [P, 8, 512], F32))
        ps_hT = [ps[:, k, 0:C] for k in range(2)]
        ps_l = [ps[:, 2 + k, 0:2 * C] for k in range(4)]
        ps_a, ps_id = ps[:, 6, 0:NBLK], ps[:, 7, 0:IDC]
        ps_start, ps_total = ps[0:ROWS, 7, 0:1], ps[:, 7, 1:2]
        ps_w = [ps[:, 2 * s:2 * s + 2, :].rearrange("p k (t c) -> p (k t) c", c=C) for s in range(2)]
        ps_z, ps_x = ps[:, 4, :], ps[:, 5, :]
        ps_s = [ps[:, 6 + s, 0:FC * WIN].rearrange("p (c n) -> p c n", c=FC) for s in range(2)]
        def ps_e(s, j):
            return ps[:, 3 * s + j // 3, (j % 3) * (C + 1):(j % 3 + 1) * (C + 1)]

        s_x, s_at, s_dist, s_dst, s_src, s_attr = (sem(n) for n in ("x_in", "at_in", "dist_in", "dst_in", "src_in", "attr_in"))
        s_wraw, s_wz, s_tail, s_lfree = sem("weights_in"), sem("weights_zeroed"), sem("tails_zeroed"), sem("l_rows_stored")
        s_const, s_pool, s_dve, s_act = sem("consts"), sem("pool_step"), sem("dve_step"), sem("act_step")
        s_recp, s_reca, s_recd = sem("rec_src_dst"), sem("rec_dist_attr"), sem("rec_cnt")
        s_rtab, s_ltab = sem("rec_tab_written"), sem("l1_tab_written")
        s_mean, s_atT, s_ain, s_var, s_std, s_norm = (sem(n) for n in ("mean_ready", "attr_T", "attr_scaled", "var_ready", "std_ready", "norm_ready"))
        s_h, s_hTp, s_hT, s_lp, s_lsb, s_base = (sem(n) for n in ("h_ready", "hT_psum", "hT_ready", "l_psum", "l_ready", "base_ready"))
        s_wdone = sem("weights_ready")
        s_cnt, s_pre, s_off, s_ends, s_ebase = (sem(n) for n in ("row_counts", "row_starts", "rows_free", "ends_marked", "edge_base_ready"))
        s_ln, s_ide2, s_hotid, s_idp, s_ide, s_nb, s_ids = (sem(n) for n in ("ln_turn", "ids_none", "edge_no_ready", "ids_psum", "ids_psum_read", "nbody_ready", "ids_ready"))
        s_zero, s_hot16 = sem("agg_zeroed"), sem("hot16_ready")
        s_idg, s_rc = sem("ids_g_ready"), sem("rec_copied")
        s_rec = [sem("rec_in0"), sem("rec_in1")]
        s_gat = [sem("gath_in0"), sem("gath_in1")]
        s_frac, s_sin, s_rbf, s_rT, s_rbfT = (sem(n) for n in ("frac_ready", "sin_ready", "rbf_ready", "rbfT_psum", "rbfT_ready"))
        s_z1, s_h1, s_z2, s_h2, s_w = (sem(n) for n in ("z1_ready", "h1_ready", "z2_ready", "h2_ready", "w_ready"))
        s_diag, s_bc, s_win = sem("diag_ready"), sem("windows_psum"), sem("windows_ready")
        s_far, s_pe, s_cut, s_msgc, s_ed, s_msg, s_hot, s_sum, s_add = (sem(n) for n in ("far_step_dve", "pe_step", "cut_steps", "msg_count_ready", "out_step", "msg_ready", "hot_ready", "sum_psum", "sum_added"))
        s_whot, s_wsum, s_wadd, s_wdve = (sem(n) for n in ("far_hot", "far_sum", "far_added", "far_step"))
        s_crow, s_cT, s_cn, s_ec, s_aggd, s_ab, s_eb, s_ap, s_al, s_fin, s_out = (sem(n) for n in ("cnt_rows_in", "cnt_T", "cnt_ready", "cnt_step", "agg_done", "aggb_ready", "out_psum", "alpha_pre", "alpha_ready", "out_ready", "out_written"))

        half = HID
        weight_loads = [(wl[0:MUL, 0:MUL], lin1_ws), (wsc[0:MUL, 0:MUL], sc_ws)]
        for m in range(3):
            weight_loads += [(wl[MUL + m:C:3, MUL + MUL * m:2 * MUL + MUL * m], lin1_wv),
                             (wsc[MUL + m:C:3, MUL + MUL * m:2 * MUL + MUL * m], sc_wv)]
        for t in range(G):
            weight_loads.append((w1[RBF * t:RBF * t + RBF, t // 2, half * (t % 2):half * (t % 2) + half], fc_w1))
        for k in range(2):
            weight_loads += [(w2[half * k:half * k + half, half * k:half * k + half], fc_w2),
                             (w3r[half * k:half * k + half, k, :], fc_w3),
                             (wv2[half * k:half * k + half, :], lin2_wv)]
        weight_loads += [(wagg[0:2 * MUL, 0, 0:MUL], lin2_ws), (wagg[0:2 * MUL, 0, C:C + 1], alpha_w)]
        WZ = 6
        NCONST = 8 + 2 * RBF
        NWL = len(weight_loads)

        block = ctx.enter_context(nc.Block())

        @block.sync
        def _(sp):
            nlast = (NBLK - 1) * P
            for lo, hi in ((0, RA), (RA, ROWS)):
                sp.dma_start(work[lo:hi, CW:CW + LEN].bitcast(I32), dst.rearrange("(p e) -> p e", p=ROWS)[lo:hi, :]).then_inc(s_dst, 16)
                sp.dma_start(work[lo:hi, 0:LEN], edge_weight.rearrange("(p e) -> p e", p=ROWS)[lo:hi, :]).then_inc(s_dist, 16)
            sp.wait_ge(s_tail, 2)
            sp.dma_start(at_rows[0:NBLK - 1, :], node_vec1[0:nlast, :].rearrange("(b p) c -> b (p c)", p=P)).then_inc(s_at, 16)
            sp.dma_start(at_rows[NBLK - 1:NBLK, 0:TAIL], node_vec1[nlast:N, :].rearrange("(a p) c -> a (p c)", a=1)).then_inc(s_at, 16)
            sp.dma_start(base[:, 0:NBLK - 1, :], x[0:nlast, :].rearrange("(b p) c -> p b c", p=P)).then_inc(s_x, 16)
            sp.dma_start(base[0:TAIL, NBLK - 1, :], x[nlast:N, :]).then_inc(s_x, 16)
            for lo, hi in ((0, RA), (RA, ROWS)):
                sp.dma_start(work[lo:hi, 2 * CW:2 * CW + LEN].bitcast(I32), src.rearrange("(p e) -> p e", p=ROWS)[lo:hi, :]).then_inc(s_src, 16)
                sp.dma_start(big[lo:hi, (LEN + 1) * REC:(LEN + 1) * REC + 4 * LEN],
                             edge_attr_4.rearrange("(p e) f -> p (e f)", p=ROWS)[lo:hi, :]).then_inc(s_attr, 16)
            sp.wait_ge(s_wz, WZ)
            for n, (to, of) in enumerate(weight_loads):
                sp.dma_start(to, of).then_inc(s_wraw, 16)
            sp.wait_ge(s_recp, 2)
            sp.wait_ge(s_reca, 2)
            sp.wait_ge(s_recd, 1)
            tab = rec_tab[0:E, :].rearrange("(p e) f -> p (e f)", p=ROWS)
            for lo, hi in ((0, RA), (RA, ROWS)):
                sp.dma_start(tab[lo:hi, :], big[lo:hi, 0:LEN * REC]).then_inc(s_rtab, 16)
            sp.dma_start(rec_tab[E:E + 1, :], big[ROWS - 1:ROWS, LEN * REC:(LEN + 1) * REC]).then_inc(s_rtab, 16)
            l1_v = l1_tab.rearrange("(b p) c -> p b c", p=P)
            sp.sem_inc(s_lfree, 2)
            with sp.Fori(0, NI) as i:
                sp.wait_ge(s_lsb, BI * i + BI + 1)
                sp.dma_start(l1_v[:, bass.ds(BI * i, BI), :], lsb[:, bass.ds(i % 2 * BI, BI), 0:C]).then_inc(s_ltab, 16)
                sp.wait_ge(s_ltab, 16 * i + 16)
                sp.sem_inc(s_lfree, 1)
            sp.wait_ge(s_aggd, 1)
            for k in range(2):
                sp.dma_start(cnt_rows[:, k, :], agg[k:k + 1, 2, 0:NBLK * P].rearrange("a (b p) -> a b p", p=P)).then_inc(s_crow, 16)
            out_v = out[0:nlast, :].rearrange("(b p) c -> p b c", p=P)
            with sp.Fori(0, NI - 1) as i:
                sp.wait_ge(s_fin, i + 1)
                sp.dma_start(out_v[:, bass.ds(BI * i, BI), :], base[:, bass.ds(BI * i, BI), :]).then_inc(s_out, 16)
            sp.wait_ge(s_fin, NI)
            sp.dma_start(out_v[:, BI * (NI - 1):NBLK - 1, :], base[:, BI * (NI - 1):NBLK - 1, :]).then_inc(s_out, 16)
            sp.dma_start(out[nlast:N, :], base[0:TAIL, NBLK - 1, :]).then_inc(s_out, 16)
            sp.wait_ge(s_out, 16 * (NI + 1))

        @block.gpsimd
        def _(po):
            nc.gpsimd.memset(base[:, NBLK - 1, :], 0.0).then_inc(s_tail, 1)
            nc.gpsimd.iota(place1, pattern=[[1, LEN]], base=1, channel_multiplier=0,
                           allow_small_or_imprecise_dtypes=True).then_inc(s_const, 1)
            for m in (wl[:, :], wsc[:, :], w1[:, :, :], w2[:, :], w3r[:, :, :], wagg[:, :, :]):
                nc.gpsimd.memset(m, 0.0).then_inc(s_wz, 1)
            nc.gpsimd.memset(ones[:, :], 1.0).then_inc(s_const, 1)
            nc.gpsimd.memset(half_pi[:, :], pi / 2).then_inc(s_const, 1)
            nc.gpsimd.memset(move, 0).then_inc(s_const, 1)
            nc.gpsimd.memset(cnt16[:, :, :], 0.0).then_inc(s_const, 1)
            nc.gpsimd.memset(ident[:, :], 0.0).then_inc(s_pool, 1)
            nc.gpsimd.memset(tri[:, :], 1.0).then_inc(s_pool, 1)
            po.wait_ge(s_pool, 2)
            nc.gpsimd.affine_select(out=ident[:, :], in_=ident[:, :], compare_op=ALU.not_equal, fill=1.0,
                                    base=0, pattern=[[-1, P]], channel_multiplier=1).then_inc(s_const, 1)
            nc.gpsimd.affine_select(out=tri[:, :], in_=tri[:, :], compare_op=ALU.is_gt, fill=0.0,
                                    base=0, pattern=[[1, P]], channel_multiplier=-1).then_inc(s_const, 1)
            nc.gpsimd.iota(iota[:, :], pattern=[[1, WIN]], base=0, channel_multiplier=0,
                           allow_small_or_imprecise_dtypes=True).then_inc(s_const, 1)
            for k in range(RBF):
                nc.gpsimd.memset(kturn[:, k:k + 1], (k + 1) / (2 * CUTOFF)).then_inc(s_const, 1)
                nc.gpsimd.memset(kfreq[:, k:k + 1], (k + 1) * pi / CUTOFF).then_inc(s_const, 1)
            po.wait_ge(s_src, 32)
            nc.gpsimd.tensor_copy(rec_rows[:, 0:LEN, SRC:SRC + 1].rearrange("p e f -> p (e f)"), src_raw.bitcast(I32)).then_inc(s_recp, 1)
            po.wait_ge(s_ends, 1)
            nc.gpsimd.tensor_copy(rec_rows[:, 0:LEN, DST:DST + 1].rearrange("p e f -> p (e f)"), dst_f[:, 0:LEN]).then_inc(s_recp, 1)
            po.wait_ge(s_recp, 1)
            nc.gpsimd.iota(edge_base, pattern=[[1, W]], base=1 - PAD, channel_multiplier=LEN,
                           allow_small_or_imprecise_dtypes=True).then_inc(s_ebase, 1)
            po.wait_ge(s_reca, 1)
            po.wait_ge(s_off, 1)
            nc.gpsimd.iota(tile_no, pattern=[[1, P // 8 + IDW]], base=-(P // 8), channel_multiplier=0,
                           allow_small_or_imprecise_dtypes=True).then_inc(s_ebase, 1)
            po.sem_inc(s_base, 2)
            with po.Fori(0, NI) as i:
                po.wait_ge(s_lsb, BI * i + BI + 1)
                nc.gpsimd.tensor_tensor(base[:, bass.ds(BI * i, BI), :], base[:, bass.ds(BI * i, BI), :],
                                        lsb[:, bass.ds(i % 2 * BI, BI), C:2 * C], ALU.add).then_inc(s_base, 1)
            def gather_records(s):
                for t in range(G):
                    po.indirect_dma_start(rec[:, s, t, :], None, rec_tab,
                                          bass.IndirectOffsetOnAxis(ids_g[:, s, t:t + 1], 0)).then_inc(s_rec[s], 16)

            def gather_sources(s):
                for t in range(G):
                    po.indirect_dma_start(gath[:, s, t, :], None, l1_tab,
                                          bass.IndirectOffsetOnAxis(src_g[:, s, t:t + 1], 0)).then_inc(s_gat[s], 16)

            po.wait_ge(s_ltab, 16 * NI)
            po.wait_ge(s_nb, 1)
            turns_n = po.value_load(nbody[0:1, 0:1], min_val=1, max_val=NBODY)
            po.wait_ge(s_idg, 1)
            gather_records(0)
            po.wait_ge(s_idg, 2)
            gather_records(1)

            def edge_turn(i):
                for s in range(2):
                    g = 2 * i + s
                    po.wait_ge(s_rc, g + 2)
                    po.sem_inc(s_pool)
                    po.wait_ge(s_msg, g + 1)
                    po.sem_inc(s_pool)
                    gather_sources(s)
                    po.wait_ge(s_idg, g + 3)
                    po.sem_inc(s_pool)
                    gather_records(s)

            with po.Fori(0, TURNS_OUT) as o:
                with po.If(TURNS_IN * o < turns_n):
                    with po.Fori(0, TURNS_IN) as k:
                        i = TURNS_IN * o + k
                        with po.If(i < turns_n):
                            edge_turn(i)
                    po.sem_inc(s_pool)

        @block.scalar
        def _(act):
            act.wait_ge(s_dist, 32)
            nc.scalar.activation(rec_rows[:, 0:LEN, 0:1].rearrange("p e f -> p (e f)"), dist, ACT.Copy).then_inc(s_reca, 1)
            act.wait_ge(s_attr, 32)
            nc.scalar.activation(rec_rows[:, 0:LEN, SH:SH + 4], attr_rows.rearrange("p (e f) -> p e f", f=4), ACT.Copy).then_inc(s_reca, 1)
            act.wait_ge(s_atT, 1)
            nc.scalar.activation(a_in[:, :], ps_a, ACT.Copy, scale=1.0 / sqrt(MUL)).then_inc(s_ain, 1)
            nc.scalar.activation(a_agg[:, :], ps_a, ACT.Copy, scale=1.0 / sqrt(2 * MUL)).then_inc(s_ain, 1)
            act.wait_ge(s_wraw, 16 * NWL)
            nc.scalar.activation(wl[:, C:C + MUL], wsc[:, 0:MUL], ACT.Copy).then_inc(s_wdone, 1)
            nc.scalar.activation(wl[:, C + MUL:2 * C].rearrange("p (o m) -> p m o", m=3),
                                 wsc[:, MUL:C].rearrange("p (m o) -> p m o", m=3), ACT.Copy).then_inc(s_wdone, 1)
            for m in range(3):
                k = m + 1
                rows = slice(HID * (k % 2), HID * (k % 2) + HID)
                nc.scalar.activation(wagg[rows, k // 2, MUL:C].rearrange("p (o m) -> p m o", m=3)[:, m, :],
                                     wv2[rows, :], ACT.Copy).then_inc(s_wdone, 1)
            act.wait_ge(s_var, 1)
            nc.scalar.activation(std[:, :], rstd[:, :], ACT.Sqrt).then_inc(s_std, 1)
            act.wait_ge(s_norm, 1)
            act.wait_ge(s_reca, 2)
            act.wait_ge(s_ain, 2)
            act.wait_ge(s_mean, 1)
            act.sem_inc(s_hT, 1)
            act.sem_inc(s_lsb, 1)
            with act.Fori(0, NI) as i:
                for j in range(BI + 2):
                    if j < BI:
                        b = BI * i + j
                        nc.scalar.activation(hbuf[:, j, :], base[:, bass.ds(b, 1), :].rearrange("p a c -> p (a c)"), ACT.Relu,
                                             bias=nmean[:, bass.ds(b, 1)]).then_inc(s_h, 1)
                    if 1 <= j <= BI:
                        act.wait_ge(s_hTp, BI * i + j)
                        nc.scalar.activation(hT[:, j - 1, :], ps_hT[(j - 1) % 2], ACT.Copy).then_inc(s_hT, 1)
                    if j >= 2:
                        act.wait_ge(s_lp, BI * i + j - 1)
                        if j == 2:
                            act.wait_ge(s_lfree, i + 1)
                            act.wait_ge(s_base, i + 1)
                        nc.scalar.activation(lsb[:, bass.ds(i % 2 * BI + (j - 2), 1), :].rearrange("p a c -> p (a c)"), ps_l[(j - 2) % 4], ACT.Copy,
                                             scale=a_norm[:, bass.ds(BI * i + j - 2, 1)]).then_inc(s_lsb, 1)
            act.wait_ge(s_nb, 1)
            turns_n = act.value_load(nbody[0:1, 0:1], min_val=1, max_val=NBODY)
            act.wait_ge(s_ids, 1)

            def edge_numbers(g, s):
                nc.scalar.activation(ids_g[:, s, :], ids[:, bass.ds(G * g, G)], ACT.Copy).then_inc(s_idg, 1)

            def mlp(g):
                act.wait_ge(s_frac, g + 1)
                nc.scalar.activation(sinv[:, :, :], frac[:, :, :], ACT.Sin, scale=2 * pi)
                nc.scalar.activation(cosv[:, :], d6[:, :], ACT.Sin, scale=-pi / (2 * CUTOFF), bias=half_pi[:, 0:1]).then_inc(s_sin, 1)
                act.wait_ge(s_rT, g + 1)
                nc.scalar.activation(rbfT[:, :], ps_z[0:RBF * G, 0:P], ACT.Copy).then_inc(s_rbfT, 1)
                act.wait_ge(s_z1, g + 1)
                nc.scalar.activation(h1[:, :], ps_z, ACT.Silu, scale=1.0 / sqrt(RBF)).then_inc(s_h1, 1)
                act.wait_ge(s_z2, g + 1)
                nc.scalar.activation(h2[:, :], ps_z, ACT.Silu, scale=1.0 / sqrt(HID)).then_inc(s_h2, 1)

            def next_numbers(g, s, i):
                act.wait_ge(s_rec[s], GIN * i + GIN)
                edge_numbers(g + 2, s)

            def hot_copy(g, s):
                act.wait_ge(s_hot, g + 1)
                nc.scalar.activation(hot16[:, :, :], hot[:, s, :, :], ACT.Copy).then_inc(s_hot16, 1)

            edge_numbers(0, 0)
            edge_numbers(1, 1)
            for s in range(2):
                next_numbers(s, s, 0)
                mlp(s)
            hot_copy(0, 0)

            def edge_turn(i):
                for s in range(2):
                    g = 2 * i + s + 2
                    next_numbers(g, s, i + 1)
                    mlp(g)
                    hot_copy(g - 1, 1 - s)

            with act.Fori(0, TURNS_OUT) as o:
                with act.If(TURNS_IN * o < turns_n):
                    with act.Fori(0, TURNS_IN) as k:
                        i = TURNS_IN * o + k
                        with act.If(i < turns_n):
                            edge_turn(i)
                    act.sem_inc(s_act, 1)

            act.wait_ge(s_aggd, 1)

            def sums_out(i, s, first):
                if not first:
                    act.wait_ge(s_eb, i - 1)
                nc.scalar.activation(aggb[s], agg[:, 0:2, bass.ds(BI * P * i, BI * P)], ACT.Copy).then_inc(s_ab, 1)

            def gate(i, s):
                act.wait_ge(s_ap, i + 1)
                nc.scalar.activation(alpha[:, s, :], apre[:, s, :], ACT.Tanh).then_inc(s_al, 1)

            act.wait_ge(s_cT, 1)
            nc.scalar.activation(cnt_n[:, :], ps_a, ACT.Copy).then_inc(s_cn, 1)
            sums_out(0, 0, True)
            sums_out(1, 1, True)
            gate(0, 0)
            sums_out(2, 0, False)
            with act.Fori(0, (NI - 3) // 2) as i:
                for s in range(2):
                    gate(2 * i + 1 + s, 1 - s)
                    sums_out(2 * i + 3 + s, 1 - s, False)
            gate(NI - 2, 1)
            gate(NI - 1, 0)

        @block.vector
        def _(dve):
            v = nc.vector
            step = [0]

            def did(ins):
                step[0] += 1
                ins.then_inc(s_dve, 1)
                return step[0]

            def link(ins):
                dve.wait_ge(s_dve, did(ins))

            v.memset(at_rows[:, :], 0.0).then_inc(s_tail, 1)
            dve.wait_ge(s_dst, 32)
            did(v.tensor_copy(dst_f[:, 0:LEN], dst_raw.bitcast(I32)))
            did(v.memset(dst_f[:, LEN:LEN + 1], -1.0))
            did(v.memset(run_start[:, 0:1], 0.0))
            did(v.memset(listed[:, LEN:LEN + 1], 0.0))
            dve.wait_ge(s_dve, step[0])
            v.tensor_tensor(listed[:, 0:LEN], dst_f[:, 0:LEN], dst_f[:, 1:LEN + 1], ALU.not_equal).then_inc(s_ends, 1)
            dve.wait_ge(s_ends, 1)
            dve.wait_ge(s_const, NCONST)
            link(v.tensor_tensor(end_mark, listed[:, 0:LEN], place1, ALU.mult))
            link(v.tensor_tensor_scan(out=run_start[:, 1:LEN + 1], data0=end_mark, data1=end_mark, initial=0.0, op0=ALU.max, op1=ALU.max))
            dve.wait_ge(s_dist, 32)
            dve.wait_ge(s_reca, 1)
            link(v.scalar_tensor_tensor(out=near, in0=dist, scalar=CUTOFF, in1=place1, op0=ALU.is_le, op1=ALU.mult))
            did(v.tensor_tensor_scan(out=near_last, data0=near, data1=near, initial=0.0, op0=ALU.max, op1=ALU.max))
            link(v.scalar_tensor_tensor(out=temp[:, 0:LEN], in0=run_start[:, 0:LEN], scalar=1.0, in1=listed[:, 0:LEN], op0=ALU.add, op1=ALU.mult))
            link(v.tensor_tensor(listed[:, 0:LEN], temp[:, 0:LEN], near_last, ALU.is_gt))
            link(v.scalar_tensor_tensor(out=listed[:, 0:LEN], in0=near, scalar=0.0, in1=listed[:, 0:LEN], op0=ALU.is_gt, op1=ALU.max))
            link(v.tensor_scalar(temp, listed, -1.0, 1.0, ALU.mult, ALU.add))
            link(v.tensor_tensor_scan(out=run_end[:, ::-1], data0=temp[:, 1:LEN + 1][:, ::-1], data1=end_mark[:, ::-1],
                                      initial=0.0, op0=ALU.mult, op1=ALU.add))
            link(v.tensor_tensor_scan(out=rank, data0=listed[:, 0:LEN], data1=listed[:, 0:LEN], initial=0.0, op0=ALU.add, op1=ALU.max))
            v.tensor_copy(tile0_f[:, :], rank[:, LEN - 1:LEN]).then_inc(s_cnt, 1)
            did(v.tensor_tensor(rec_rows[:, 0:LEN, CNT:CNT + 1].rearrange("p e f -> p (e f)"), run_end, run_start[:, 0:LEN], ALU.subtract))
            link(v.memset(rec_rows[:, LEN, :], 0.0))
            did(v.memset(rec_rows[:, LEN, 0:1], 8 * CUTOFF))
            v.tensor_copy(rec_rows[:, LEN, DST:DST + 1], dst_f[:, LEN - 1:LEN]).then_inc(s_recd, 1)

            dve.wait_ge(s_x, 32)
            k0, LNS = step[0], 2 * BI + 1
            with dve.Fori(0, NI) as i:
                for j in range(BI):
                    if j == 0:
                        dve.wait_ge(s_dve, LNS * i + k0)
                    v.bn_stats(stats[:, j, :], base[:, bass.ds(BI * i + j, 1), :].rearrange("p a c -> p (a c)")).then_inc(s_dve, 1)
                dve.wait_ge(s_dve, LNS * i + k0 + BI)
                dve.sem_inc(s_ln, 1)
                for j in range(BI):
                    v.bn_aggr(mv7[:, j, :], stats[:, j, :]).then_inc(s_dve, 1)
                dve.wait_ge(s_dve, LNS * i + k0 + 2 * BI)
                v.tensor_copy(mv[:, bass.ds(BI * i, BI), :], mv7[:, :, :]).then_inc(s_dve, 1)
            step[0] += LNS * NI
            dve.wait_ge(s_dve, step[0])
            v.tensor_scalar(nmean[:, :], mv[:, :, 0], -1.0, None, ALU.mult).then_inc(s_mean, 1)
            v.tensor_scalar(rstd[:, :], mv[:, :, 1], EPS, None, ALU.add).then_inc(s_var, 1)
            dve.wait_ge(s_std, 1)
            link(v.reciprocal(rstd[:, :], std[:, :]))
            dve.wait_ge(s_ain, 2)
            v.tensor_tensor(a_norm[:, :], a_in[:, :], rstd[:, :], ALU.mult).then_inc(s_norm, 1)

            dve.wait_ge(s_pre, 1)
            link(v.tensor_copy(base_i[:, :], ps_start))
            did(v.tensor_single_scalar(tile0_i[:, :], base_i[:, :], 7, ALU.logical_shift_right))
            did(v.tensor_single_scalar(off_i[:, :], base_i[:, :], P - 1, ALU.bitwise_and))
            link(v.tensor_scalar(tot_i[:, :], ps_total, float(BODY * P - 1), None, ALU.add))
            did(v.tensor_copy(tile0_f[:, :], tile0_i[:, :]))
            link(v.tensor_copy(off_f[:, :], off_i[:, :]))
            v.tensor_single_scalar(nbody[:, :], tot_i[:, :], 11, ALU.logical_shift_right).then_inc(s_nb, 1)
            did(v.tensor_scalar(pad_off[:, :], off_f[:, :], -1.0, float(PAD), ALU.mult, ALU.add))
            link(v.tensor_tensor(shift0, place1, rank, ALU.subtract))
            did(v.memset(sh_a[:, 0:PAD], 0))
            did(v.memset(sh_a[:, PAD + LEN:W], 0))
            dve.wait_ge(s_dve, step[0])
            v.scalar_tensor_tensor(out=sh_a[:, PAD:PAD + LEN], in0=shift0, scalar=pad_off[:, 0:1], in1=listed[:, 0:LEN],
                                   op0=ALU.add, op1=ALU.mult).then_inc(s_off, 1)
            dve.wait_ge(s_off, 1)

            now, new = sh_a, sh_b
            for k in range(STEPS):
                link(v.tensor_scalar(stay, now, k, 1, ALU.logical_shift_right, ALU.bitwise_and))
                link(v.tensor_tensor(move[:, 0:W], stay, now, ALU.mult))
                link(v.tensor_tensor(stay, now, move[:, 0:W], ALU.subtract))
                link(v.tensor_tensor(new, stay, move[:, 2 ** k:2 ** k + W], ALU.add))
                now, new = new, now

            dve.wait_ge(s_ebase, 2)
            dve.wait_ge(s_recp, 2)
            n = did(v.scalar_tensor_tensor(out=edge_no, in0=now, scalar=0.0, in1=edge_base, op0=ALU.is_gt, op1=ALU.mult))
            link(v.tensor_scalar(tile_hot, tile_no, tile0_f[:, 0:1], None, ALU.is_equal))
            v.tensor_tensor(edge_no, edge_no, now, ALU.add).then_inc(s_hotid, 1)
            dve.wait_ge(s_wraw, 16 * NWL)
            did(v.tensor_scalar(w3[:, :, 0:3 * MUL], w3r[:, :, 0:3 * MUL], 1.0 / sqrt(HID), None, ALU.mult))
            did(v.tensor_scalar(w3[:, :, 3 * MUL:C], w3r[:, :, 3 * MUL:C], 1.0 / sqrt(HID) / sqrt(3.0), None, ALU.mult))
            dve.wait_ge(s_nb, 1)
            turns_n = dve.value_load(nbody[0:1, 0:1], min_val=1, max_val=NBODY)

            def ids_out(c):
                dve.wait_ge(s_idp, c + 1)
                link(v.tensor_scalar(none[:, :], ps_id, 0.0, float(E + 1), ALU.is_equal, ALU.mult))
                v.scalar_tensor_tensor(out=ids[:, IDC * c:IDC * (c + 1)], in0=ps_id, scalar=-1.0, in1=none[:, :],
                                       op0=ALU.add, op1=ALU.add).then_inc(s_ide, 1)
                dve.wait_ge(s_ide, c + 1)

            ids_out(0)
            for c in range(1, NIDC):
                with dve.If(turns_n > IDC // BODY * c - 2):
                    dve.wait_ge(s_idp, c + 1)
                    v.tensor_scalar(none[:, :], ps_id, 0.0, float(E + 1), ALU.is_equal, ALU.mult).then_inc(s_ide2, 1)
                    dve.wait_ge(s_ide2, c)
                    v.scalar_tensor_tensor(out=ids[:, IDC * c:IDC * (c + 1)], in0=ps_id, scalar=-1.0, in1=none[:, :],
                                           op0=ALU.add, op1=ALU.add).then_inc(s_ide, 1)
                    dve.wait_ge(s_ide, c + 1)
            dve.sem_inc(s_ids, 1)

            sh = [recw[:, s, :, SH:SH + 4] for s in range(2)]
            K1, K2, K3 = 12, 5, 8
            L1 = step[0]
            PER = K1 + K2 + K3

            class Steps:
                def __init__(self, start):
                    self.start, self.n = start, 0

                def did(self, ins):
                    self.n += 1
                    ins.then_inc(s_dve, 1)
                    return self.n

                def need(self, n):
                    dve.wait_ge(s_dve, self.start + n)

            one64 = ones[:, 0:G * RBF].rearrange("p (t k) -> p t k", t=G)

            def radial(g, s, i, own, first=False):
                dve.wait_ge(s_rec[s], GIN * i + GIN)
                own.did(v.tensor_copy(recw[:, s, :, :], rec[:, s, :, :]))
                a = own.did(v.tensor_scalar(d6[:, :], rec[:, s, :, 0], CUTOFF, None, ALU.min))
                v.tensor_copy(src_g[:, s, :], rec[:, s, :, SRC]).then_inc(s_rc, 1)
                own.need(a)
                dm = d6[:, :].unsqueeze(2).broadcast_to([P, G, RBF])
                a = own.did(v.tensor_tensor(turns[:, :, :], dm, kturn[:, :].unsqueeze(1).broadcast_to([P, G, RBF]), ALU.mult))
                b = own.did(v.tensor_tensor(fd[:, :, :], dm, kfreq[:, :].unsqueeze(1).broadcast_to([P, G, RBF]), ALU.mult))
                own.need(a)
                a = own.did(v.tensor_scalar(whole[:, :, :], turns[:, :, :], ROUND, ROUND, ALU.add, ALU.subtract))
                own.need(b)
                b = own.did(v.scalar_tensor_tensor(out=rfd[:, :, :], in0=fd[:, :, :], scalar=-1.0, in1=fd[:, :, :], op0=ALU.mult, op1=ALU.max))
                own.need(b)
                own.did(v.tensor_scalar(small[:, :, :], rfd[:, :, :], SMALL, None, ALU.is_lt))
                own.need(own.n)
                v.tensor_tensor(frac[:, :, :], turns[:, :, :], whole[:, :, :], ALU.subtract).then_inc(s_frac, 1)
                own.did(v.copy_predicated(fd[:, :, :], small[:, :, :], one64))
                if not first:
                    dve.wait_ge(s_rT, g)
                own.did(v.tensor_copy(dst_c[:, :], recw[:, s, :, DST]))

            def basis(g, s, own):
                own.need(own.n)
                a = own.did(v.reciprocal(rfd[:, :, :], fd[:, :, :]))
                dve.wait_ge(s_sin, g + 1)
                own.need(a)
                a = own.did(v.tensor_tensor(cut2[:, :], cosv[:, :], cosv[:, :], ALU.mult))
                b = own.did(v.tensor_tensor(rb[:, :, :], sinv[:, :, :], rfd[:, :, :], ALU.mult))
                own.need(b)
                v.scalar_tensor_tensor(out=cut[:, :], in0=recw[:, s, :, 0], scalar=CUTOFF, in1=cut2[:, :],
                                       op0=ALU.is_le, op1=ALU.mult).then_inc(s_cut, 1)
                v.copy_predicated(rb[:, :, :], small[:, :, :], one64).then_inc(s_cut, 1)
                dve.wait_ge(s_cut, 2 * g + 2)
                v.tensor_tensor(rbf[:, :].rearrange("p (t k) -> p t k", t=G), rb[:, :, :],
                                cut[:, :].unsqueeze(2).broadcast_to([P, G, RBF]), ALU.mult).then_inc(s_rbf, 1)

            def extent(g, own):
                dve.wait_ge(s_rT, g + 1)
                own.did(v.tensor_reduce(minmax[:, 0:1], ps_x[0:G, P:2 * P], AX_X, ALU.min))
                a = own.did(v.tensor_reduce(minmax[:, 1:2], ps_x[0:G, P:2 * P], AX_X, ALU.max))
                own.need(a)
                v.tensor_tensor(diag[:, :, :], ident[0:G, 0:G].unsqueeze(1).broadcast_to([G, 2, G]),
                                minmax[:, :].unsqueeze(2).broadcast_to([G, 2, G]), ALU.mult).then_inc(s_diag, 1)

            def windows(g, s, own):
                dve.wait_ge(s_bc, g + 1)
                lows = ps_x[:, 2 * P:2 * P + G].rearrange("p (q t) -> p q t", t=2)
                highs = ps_x[:, 2 * P + G:2 * P + 2 * G].rearrange("p (q t) -> p q t", t=2)
                own.did(v.tensor_reduce(win0[:, :], lows, AX_X, ALU.min))
                a = own.did(v.tensor_reduce(winmax[:, :], highs, AX_X, ALU.max))
                own.need(a)
                a = own.did(v.tensor_tensor(span4[:, :], winmax[:, :], win0[:, :], ALU.subtract))
                v.tensor_copy(win0_i[:, s, :], win0[:, :]).then_inc(s_win, 1)
                v.tensor_tensor(dloc[:, s, :].rearrange("p (q t) -> p q t", t=2),
                                recw[:, s, :, DST].rearrange("p (q t) -> p q t", t=2),
                                win0[:, :].unsqueeze(2).broadcast_to([P, NPAIR, 2]), ALU.subtract).then_inc(s_win, 1)
                own.need(a)
                v.tensor_reduce(span_i[:, s:s + 1], span4[:, :], AX_X, ALU.max).then_inc(s_win, 1)

            def messages(g, s, i, own):
                gs, gv = gath[:, s, :, 0:MUL], gath[:, s, :, MUL:C].rearrange("p t (m c) -> p t m c", m=3)
                w = ps_w[s]
                shm = sh[s][:, :, 1:4].unsqueeze(3).broadcast_to([P, G, 3, MUL])
                dve.wait_ge(s_gat[s], GIN * i + GIN)
                ga = own.did(v.tensor_tensor(gsh0[:, :, :], gath[:, s, :, :], sh[s][:, :, 0:1].broadcast_to([P, G, C]), ALU.mult))
                tv = own.did(v.tensor_tensor(gsh1[:, :, :, :], gv, shm, ALU.mult))
                dve.wait_ge(s_w, g + 1)
                tt = own.did(v.tensor_tensor(t01[:, :, :], gs, w[:, :, MUL:2 * MUL], ALU.mult))
                own.need(tv)
                d1 = own.did(v.tensor_tensor(dot1[:, :, :], gsh1[:, :, 0, :], gsh1[:, :, 1, :], ALU.add))
                own.did(v.tensor_tensor(msg[:, :, 0:MUL], gsh0[:, :, 0:MUL], w[:, :, 0:MUL], ALU.mult))
                own.need(d1)
                d2 = own.did(v.tensor_tensor(dot2[:, :, :], dot1[:, :, :], gsh1[:, :, 2, :], ALU.add))
                mv_ = msg[:, :, 2 * MUL:2 * C].rearrange("p t (m k c) -> p t m k c", m=3, k=2)
                own.did(v.tensor_tensor(mv_[:, :, :, 1, :], gsh0[:, :, MUL:C].rearrange("p t (m c) -> p t m c", m=3),
                                        w[:, :, 2 * MUL:3 * MUL].unsqueeze(2).broadcast_to([P, G, 3, MUL]), ALU.mult))
                own.need(d2)
                own.did(v.tensor_tensor(msg[:, :, MUL:2 * MUL], dot2[:, :, :], w[:, :, 3 * MUL:C], ALU.mult))
                v.tensor_tensor(mv_[:, :, :, 0, :], t01[:, :, :].unsqueeze(2).broadcast_to([P, G, 3, MUL]), shm, ALU.mult).then_inc(s_msg, 1)
                v.tensor_scalar(cnt16[:, :, 0], recw[:, s, :, CNT], 0.0, None, ALU.max).then_inc(s_msgc, 1)
                dve.wait_ge(s_msgc, 2 * g + 1)
                v.scalar_tensor_tensor(out=cnt16[:, :, 1], in0=recw[:, s, :, CNT], scalar=0.0, in1=cnt16[:, :, 0],
                                       op0=ALU.max, op1=ALU.subtract).then_inc(s_msgc, 1)

            def one_hot(s):
                return v.tensor_tensor(hot[:, s, :, :], iota[:, :].unsqueeze(1).broadcast_to([P, G, WIN]),
                                       dloc[:, s, :].unsqueeze(2).broadcast_to([P, G, WIN]), ALU.is_equal)

            def add_window(q, start):
                part = agg[:, :, bass.ds(start, WIN)]
                return v.tensor_tensor(part, part, ps_s[q % 2], ALU.add)

            far_turns = dve.alloc_register("far_turns_dve")
            dve.reg_mov(far_turns, 0)

            def far_windows(g, s, span):
                dve.wait_ge(s_add, NPAIR * g + NPAIR + 2)
                dve.sem_inc(s_far, 1)
                with dve.Fori(1, FAR) as k:
                    with dve.If(span >= WIN * k):
                        turn = dve.snap(far_turns)
                        dve.wait_ge(s_whot, turn + 1)
                        v.tensor_scalar(dloc[:, s, :], dloc[:, s, :], float(WIN), None, ALU.subtract).then_inc(s_wdve, 1)
                        v.tensor_scalar(win0_i[:, s, :], win0_i[:, s, :], WIN, NBLK * P, ALU.add, ALU.min).then_inc(s_wdve, 1)
                        dve.wait_ge(s_wdve, 3 * turn + 2)
                        one_hot(s).then_inc(s_wdve, 1)
                        dve.wait_ge(s_wdve, 3 * turn + 3)
                        v.tensor_copy(hot16[:, :, :], hot[:, s, :, :]).then_inc(s_whot, 1)
                        for q in range(NPAIR):
                            start = dve.value_load(win0_i[0:1, s, q:q + 1], min_val=0, max_val=NBLK * P)
                            dve.wait_ge(s_wsum, NPAIR * turn + q + 1)
                            dve.wait_ge(s_wadd, NPAIR * turn + q + 1)
                            add_window(q, start).then_inc(s_wadd, 1)
                        dve.reg_add(far_turns, far_turns, 1)
                dve.wait_ge(s_wadd, NPAIR * dve.snap(far_turns) + 1)
                dve.sem_inc(s_far, 1)

            def one_hot_of(g, s):
                dve.wait_ge(s_win, 3 * g + 3)
                one_hot(s).then_inc(s_hot, 1)

            def add_sum(g, s, q, start):
                dve.wait_ge(s_sum, NPAIR * g + q + 1)
                dve.wait_ge(s_add, NPAIR * g + q + 2)
                add_window(q, start).then_inc(s_add, 1)

            own = Steps(L1)
            dve.sem_inc(s_rc, 1)
            dve.sem_inc(s_msg, 2)
            dve.sem_inc(s_add, 2)
            dve.sem_inc(s_whot, 1)
            dve.sem_inc(s_wadd, 1)

            def zero(c):
                if c == 0:
                    dve.wait_ge(s_rtab, 48)
                    dve.wait_ge(s_ltab, 16 * NI)
                    dve.wait_ge(s_base, NI + 2)
                v.memset(agg[:, c, :], 0.0).then_inc(s_zero, 1)

            zero(0)
            radial(0, 0, 0, own, first=True)
            basis(0, 0, own)
            extent(0, own)
            zero(1)
            windows(0, 0, own)
            one_hot_of(0, 0)
            radial(1, 1, 0, own)
            basis(1, 1, own)
            zero(2)
            dve.wait_ge(s_zero, 3)
            start0 = L1 + own.n

            def edge_turn(i):
                for s in range(2):
                    g = 2 * i + s
                    own = Steps(i * (2 * PER) + (start0 + s * PER))
                    extent(g + 1, own)
                    messages(g, s, i, own)
                    windows(g + 1, 1 - s, own)
                    one_hot_of(g + 1, 1 - s)
                    start = [dve.value_load(win0_i[0:1, s, q:q + 1], min_val=0, max_val=N - 1) for q in range(NPAIR)]
                    add_sum(g, s, 0, start[0])
                    radial(g + 2, s, i + 1, own)
                    add_sum(g, s, 1, start[1])
                    basis(g + 2, s, own)
                    add_sum(g, s, 2, start[2])
                    add_sum(g, s, 3, start[3])
                    span = dve.value_load(span_i[0:1, s:s + 1], min_val=0, max_val=N)
                    with dve.If(span >= WIN):
                        far_windows(g, s, span)
                    dve.sem_inc(s_far, 1)
                    assert own.n == PER, own.n

            with dve.Fori(0, TURNS_OUT) as o:
                with dve.If(TURNS_IN * o < turns_n):
                    with dve.Fori(0, TURNS_IN) as k:
                        i = TURNS_IN * o + k
                        with dve.If(i < turns_n):
                            edge_turn(i)
                    dve.sem_inc(s_far, 1)
            dve.wait_ge(s_add, 2 * NPAIR * turns_n + 2)
            dve.sem_inc(s_aggd, 1)

            def finish(i, s):
                own_e = EP * i
                dve.wait_ge(s_eb, i + 1)
                for k in range(3):
                    nb = min(3, BI - 3 * k)
                    v.tensor_tensor(apre[:, s, 3 * k:3 * k + nb],
                                    ps[:, 3 * s + k, 0:3 * (C + 1)].rearrange("p (b c) -> p b c", c=C + 1)[:, 0:nb, C],
                                    scale[:, bass.ds(BI * i + 3 * k, nb)], ALU.mult).then_inc(s_ap if k == 2 else s_ed, 1)
                dve.wait_ge(s_al, i + 1)
                v.tensor_tensor(salpha[:, s, :], alpha[:, s, :], scale[:, bass.ds(BI * i, BI)], ALU.mult).then_inc(s_ed, 1)
                dve.wait_ge(s_ed, own_e + 3)
                for j in range(BI):
                    to = base[:, bass.ds(BI * i + j, 1), :].rearrange("p a c -> p (a c)")
                    ins = v.scalar_tensor_tensor(out=to, in0=ps_e(s, j)[:, 0:C], scalar=salpha[:, s, j:j + 1], in1=to,
                                                 op0=ALU.mult, op1=ALU.add)
                ins.then_inc(s_fin, 1)

            EP = 3
            dve.wait_ge(s_cn, 1)
            v.tensor_scalar(cmax[:, :], cnt_n[:, :], 1.0, None, ALU.max).then_inc(s_ec, 1)
            dve.wait_ge(s_ec, 1)
            v.reciprocal(rcnt[:, :], cmax[:, :]).then_inc(s_ec, 1)
            dve.wait_ge(s_ec, 2)
            v.tensor_tensor(scale[:, :], rcnt[:, :], a_agg[:, :], ALU.mult).then_inc(s_ec, 1)
            dve.wait_ge(s_ec, 3)
            dve.wait_ge(s_base, NI + 2)
            with dve.Fori(0, (NI - 1) // 2) as i:
                finish(2 * i, 0)
                finish(2 * i + 1, 1)
            finish(NI - 1, 0)

        @block.tensor
        def _(pe):
            mm = nc.tensor.matmul
            pe.wait_ge(s_const, NCONST)
            pe.wait_ge(s_at, 32)
            nc.tensor.transpose(ps_a, at_rows[:, :], ident[0:NBLK, 0:NBLK]).then_inc(s_atT, 1)
            pe.wait_ge(s_cnt, 1)
            mm(ps_start, tri[0:ROWS, 0:ROWS], tile0_f[:, :], start=True, stop=True)
            mm(ps_total, ones[0:ROWS, :], tile0_f[:, :], start=True, stop=True).then_inc(s_pre, 1)
            pe.wait_ge(s_wdone, 5)
            with pe.Fori(0, NI) as i:
                for j in range(BI + 1):
                    if j < BI:
                        pe.wait_ge(s_h, BI * i + j + 1)
                        pe.wait_ge(s_hT, BI * i + max(j, 1))
                        nc.tensor.transpose(ps_hT[j % 2], hbuf[:, j, :], ident[:, :]).then_inc(s_hTp, 1)
                    if j >= 1:
                        pe.wait_ge(s_hT, BI * i + j + 1)
                        pe.wait_ge(s_lsb, BI * i + max(j - 4, 0) + 1)
                        mm(ps_l[(j - 1) % 4], hT[:, j - 1, :], wl[:, :], start=True, stop=True).then_inc(s_lp, 1)
            pe.wait_ge(s_hotid, 1)

            def ids_of(c):
                for k in range(LCH):
                    at = P // 8 - k + IDC * c
                    last = mm(ps_id, edge_no[:, P * k:P * (k + 1)], tile_hot[:, at:at + IDC], start=(k == 0), stop=(k == LCH - 1))
                last.then_inc(s_idp, 1)

            ids_of(0)
            pe.wait_ge(s_nb, 1)
            turns_n = pe.value_load(nbody[0:1, 0:1], min_val=1, max_val=NBODY)
            for c in range(1, NIDC):
                with pe.If(turns_n > IDC // BODY * c - 2):
                    pe.wait_ge(s_ide, c)
                    ids_of(c)
            pe.wait_ge(s_ids, 1)
            pe.wait_ge(s_lsb, NBLK + 1)

            def radial_mlp(g, s, first):
                pe.wait_ge(s_rbf, g + 1)
                nc.tensor.transpose(ps_x[0:G, P:2 * P], dst_c[:, :], ident[:, :])
                nc.tensor.transpose(ps_z[0:RBF * G, 0:P], rbf[:, :], ident[:, :]).then_inc(s_rT, 1)
                pe.wait_ge(s_rbfT, g + 1)
                for j in range(4):
                    last = mm(ps_z[:, P * j:P * (j + 1)], w1[:, j, :], rbfT[:, :], start=True, stop=True)
                last.then_inc(s_z1, 1)
                pe.wait_ge(s_h1, g + 1)
                mm(ps_z, w2[:, :], h1[:, :], start=True, stop=True).then_inc(s_z2, 1)
                pe.wait_ge(s_h2, g + 1)
                if not first:
                    pe.wait_ge(s_msg, g + 1)
                for j in range(4):
                    last = mm(ps_w[s][:, 2 * j:2 * j + 2, :], h2[:, P * j:P * (j + 1)], w3[:, :, :], start=True, stop=True)
                last.then_inc(s_w, 1)

            def spread(g):
                pe.wait_ge(s_diag, g + 1)
                mm(ps_x[:, 2 * P:2 * P + 2 * G], ones[0:G, :], diag[:, :, :], start=True, stop=True).then_inc(s_bc, 1)

            def pair_sum(q, s):
                for c in range(2):
                    for t in range(2):
                        mm(ps_s[q % 2][:, c, :], msg[:, 2 * q + t, P * c:P * (c + 1)], hot[:, s, 2 * q + t, :],
                           start=(t == 0), stop=(t == 1))
                for t in range(2):
                    last = mm(ps_s[q % 2][:, 2, :], cnt16[:, 2 * q + t, :], hot16[:, 2 * q + t, :], start=(t == 0), stop=(t == 1))
                return last

            far_turns = pe.alloc_register("far_turns_pe")
            pe.reg_mov(far_turns, 0)

            def far_windows(span, s):
                with pe.Fori(1, FAR) as k:
                    with pe.If(span >= WIN * k):
                        turn = pe.snap(far_turns)
                        pe.wait_ge(s_whot, turn + 2)
                        for q in range(NPAIR):
                            if q >= 2:
                                pe.wait_ge(s_wadd, NPAIR * turn + q)
                            pair_sum(q, s).then_inc(s_wsum, 1)
                        pe.reg_add(far_turns, far_turns, 1)

            radial_mlp(0, 0, True)
            spread(0)
            radial_mlp(1, 1, True)

            def edge_turn(i):
                for s in range(2):
                    g = 2 * i + s
                    spread(g + 1)
                    pe.wait_ge(s_hot16, g + 1)
                    pe.sem_inc(s_pe, 1)
                    pe.wait_ge(s_msgc, 2 * g + 2)
                    pe.sem_inc(s_pe, 1)
                    span = pe.value_load(span_i[0:1, s:s + 1], min_val=0, max_val=N)
                    for q in range(NPAIR):
                        pe.wait_ge(s_add, NPAIR * g + q + 1)
                        pair_sum(q, s).then_inc(s_sum, 1)
                    with pe.If(span >= WIN):
                        far_windows(span, s)
                    pe.sem_inc(s_pe, 1)
                    radial_mlp(g + 2, s, False)

            with pe.Fori(0, TURNS_OUT) as o:
                with pe.If(TURNS_IN * o < turns_n):
                    with pe.Fori(0, TURNS_IN) as k:
                        i = TURNS_IN * o + k
                        with pe.If(i < turns_n):
                            edge_turn(i)
                    pe.sem_inc(s_pe, 1)

            def project(i, s, free):
                pe.wait_ge(s_ab, i + 1)
                if free is not None:
                    pe.wait_ge(s_fin, free)
                for j in range(BI):
                    nodes = slice(P * j, P * (j + 1))
                    for c in range(2):
                        last = mm(ps_e(s, j), aggb[s][:, c, nodes], wagg[:, c, :], start=(c == 0), stop=(c == 1))
                last.then_inc(s_eb, 1)

            pe.wait_ge(s_crow, 32)
            mm(ps_a, cnt_rows[:, 0, :], ident[0:NBLK, 0:NBLK], start=True, stop=False)
            mm(ps_a, cnt_rows[:, 1, :], ident[0:NBLK, 0:NBLK], start=False, stop=True).then_inc(s_cT, 1)
            project(0, 0, None)
            project(1, 1, None)
            with pe.Fori(0, (NI - 3) // 2) as i:
                project(2 * i + 2, 0, 2 * i + 1)
                project(2 * i + 3, 1, 2 * i + 2)
            project(NI - 1, 0, NI - 2)


_INS = ['x', 'src', 'dst', 'edge_attr_4', 'edge_weight', 'node_vec1', 'L0_gnn_sc_ws', 'L0_gnn_sc_wv', 'L0_gnn_lin1_ws',
        'L0_gnn_lin1_wv', 'L0_gnn_fc_w1', 'L0_gnn_fc_w2', 'L0_gnn_fc_w3', 'L0_gnn_lin2_ws', 'L0_gnn_lin2_wv', 'L0_gnn_alpha_w']


def kernel(**inputs):
    import concourse.bacc as bacc
    from concourse.bass_utils import run_bass_kernel_spmd

    nc = bacc.Bacc("TRN2", target_bir_lowering=False, num_devices=1)
    arrays, args = {}, []
    for name in _INS:
        a = np.ascontiguousarray(inputs[name])
        arrays[f"in_{name}"] = a
        args.append(nc.dram_tensor(f"in_{name}", a.shape, mybir.dt.from_np(a.dtype), kind="ExternalInput").ap())
    args.append(nc.dram_tensor("out_x", (N, C), F32, kind="ExternalOutput").ap())
    gnn_kernel(nc, *args)
    r = run_bass_kernel_spmd(nc, [arrays], core_ids=[0])
    return r.results[0]["out_x"]
```

```python
from contextlib import ExitStack
from math import pi, sqrt

import numpy as np
import concourse.bass as bass
from concourse import mybir

F32 = mybir.dt.float32
I32 = mybir.dt.int32
I16 = mybir.dt.int16
BF16 = mybir.dt.bfloat16
ALU = mybir.AluOpType
ACT = mybir.ActivationFunctionType
AX_X = mybir.AxisListType.X

P = 128
N = 6250
C = 128
E = 200000
MUL = 32
RBF = 8
HID = 64
CUTOFF = 6.0
SMALL = 1e-6
EPS = 1e-5
ROUND = 1.5 * 2.0 ** 23

NBLK = -(-N // P)
BI = 7
NI = NBLK // BI
NI_A = 5
NI_P = 4
assert NI - 2 <= NI_A
SUM_STEPS = C.bit_length() - 1
TAIL = N - (NBLK - 1) * P

ROWS = 125
LEN = E // ROWS
RA = 112
PAD = P
W = 14 * P
CW = W + 32
STEPS = 11
LCH = W // P

G = 8
NPAIR = G // 2
GIN = 16 * G
TILES = -(-E // P)
GROUPS = -(-TILES // G)
TURNS = (64, 32, 16, 8, 4, 2, 1)
assert 2 * sum(TURNS) + 3 >= GROUPS
IDC = 2 * P
IDS = [(0, P)] + [(lo, IDC) for lo in range(P, (GROUPS + 4) * G, IDC)]
IDW = sum(IDS[-1])
REC = 8
SRC, DST, CNT, SH = 1, 2, 3, 4

FC = 3
WIN = 144
AGGW = NBLK * P + WIN + 8
FAR = -(-N // WIN)


def gnn_kernel(nc, x, src, dst, edge_attr_4, edge_weight, node_vec1, sc_ws, sc_wv, lin1_ws, lin1_wv,
               fc_w1, fc_w2, fc_w3, lin2_ws, lin2_wv, alpha_w, out):
    rec_tab = nc.dram_tensor("rec_tab", (E + 1, REC), F32, kind="Internal").ap()
    l1_tab = nc.dram_tensor("l1_tab", (NBLK * P, C), F32, kind="Internal").ap()

    ctx = ExitStack()
    with ctx:
        def sb(name, shape, dt=F32):
            return ctx.enter_context(nc.sbuf_tensor(name, shape, dt))

        def sem(name):
            return ctx.enter_context(nc.semaphore(name))

        big = sb("big", [P, FC * AGGW])
        rec_rows = big[0:ROWS, 0:(LEN + 1) * REC].rearrange("p (e f) -> p e f", f=REC)
        attr_rows = big[0:ROWS, (LEN + 1) * REC:(LEN + 1) * REC + 4 * LEN]
        at_h = 2 * AGGW
        assert (LEN + 1) * REC <= at_h and at_h + 7 * BI * C <= FC * AGGW
        centred = big[:, at_h:at_h + 2 * BI * C].rearrange("p (s b c) -> p s b c", s=2, b=BI)
        hT = big[:, at_h + 2 * BI * C:at_h + 3 * BI * C].rearrange("p (b c) -> p b c", b=BI)
        lsb = big[:, at_h + 3 * BI * C:at_h + 7 * BI * C].rearrange("p (s b c) -> p s b c", s=2, b=BI)
        agg = big[:, :].rearrange("p (c n) -> p c n", c=FC)

        work = sb("work", [P, 8 * CW + 3 * W // 2 + (W + 1024) // 2])

        def col(n, width=W):
            return work[0:ROWS, n * CW:n * CW + width]

        dist, dst_raw, src_raw, dst_f = col(0, LEN), col(1, LEN), col(2, LEN), col(3, LEN + 1)
        place1, rank, run_start, listed = col(4, LEN), col(5, LEN), col(6, LEN + 1), col(7, LEN + 1)
        near, tile_no = col(0, LEN), col(0, P // 8 + IDW)
        end_mark, shift0, tile_hot = col(1, LEN), col(1, LEN), col(1, P // 8 + IDW)
        edge_base, edge_no = col(2), col(3)
        near_last, run_end = col(5, LEN), col(0, LEN)
        at16 = 8 * CW
        sh_a = work[0:ROWS, at16:at16 + W // 2].bitcast(I16)
        sh_b = work[0:ROWS, at16 + W // 2:at16 + W].bitcast(I16)
        temp = work[0:ROWS, at16:at16 + LEN + 1]
        stay = work[0:ROWS, at16 + W:at16 + 3 * W // 2].bitcast(I16)
        move = work[0:ROWS, at16 + 3 * W // 2:at16 + 3 * W // 2 + (W + 1024) // 2].bitcast(I16)

        used = [0]

        def carve(*shape):
            n = int(np.prod(shape))
            v = work[:, used[0]:used[0] + n]
            used[0] += n
            if len(shape) == 2:
                return v.rearrange("p (a b) -> p a b", a=shape[0])
            if len(shape) == 3:
                return v.rearrange("p (a b c) -> p a b c", a=shape[0], b=shape[1])
            return v

        gath = carve(2, G, C)
        gsh0 = carve(G, C)
        gsh1 = carve(G, 3, MUL)
        t01 = carve(G, MUL)
        dot1, dot2 = carve(G, MUL), carve(G, MUL)
        msg = carve(G, 2 * C)
        hot = carve(2, G, WIN)
        hot16 = carve(G * WIN // 2).bitcast(BF16).rearrange("p (t n) -> p t n", t=G)
        aggb = [carve(2, BI * P), carve(2, BI * P)]
        assert used[0] <= 8 * CW + 3 * W // 2 + (W + 1024) // 2, used[0]

        base = sb("base", [P, NBLK, C])
        ids = sb("ids", [P, max(IDW, BI * NI_P * C // 2)], I32)
        part_sums = ids[:, 0:BI * NI_P * C // 2].bitcast(F32).rearrange("p (b c) -> p b c", c=C // 2)
        rec, recw = sb("rec", [P, 2, G, REC]), sb("recw", [P, 2, G, REC])
        ids_g, src_g = sb("ids_g", [P, 2, G], I32), sb("src_g", [P, 2, G], I32)
        rbfT, h1, h2 = sb("rbfT", [RBF * G, P]), sb("h1", [P, 4 * P]), sb("h2", [P, 4 * P])
        d6, cosv, cut2, cut = sb("d6", [P, G]), sb("cosv", [P, G]), sb("cut2", [P, G]), sb("cut", [P, G])
        turns, whole, frac = sb("turns", [P, G, RBF]), sb("whole", [P, G, RBF]), sb("frac", [P, G, RBF])
        fd, rfd, sinv = sb("fd", [P, G, RBF]), sb("rfd", [P, G, RBF]), sb("sinv", [P, G, RBF])
        small = sb("small", [P, G, RBF], I32)
        rb, rbf = sb("rb", [P, G, RBF]), sb("rbf", [P, G * RBF])
        dst_c = sb("dst_c", [P, G])
        minmax, diag = sb("minmax", [G, 2]), sb("diag", [G, 2, G])
        win0, winmax, span4 = sb("win0", [P, NPAIR]), sb("winmax", [P, NPAIR]), sb("span4", [P, NPAIR])
        win0_i, span_i = sb("win0_i", [P, 2, NPAIR], I32), sb("span_i", [P, 2], I32)
        dloc = sb("dloc", [P, 2, G])
        cnt16 = sb("cnt16", [P, G, P], BF16)

        ident, iota, tri = sb("ident", [P, P]), sb("iota", [P, WIN]), sb("tri", [P, P])
        ones, half_pi = sb("ones", [P, P]), sb("half_pi", [P, 1])
        kturn, kfreq = sb("kturn", [P, RBF]), sb("kfreq", [P, RBF])
        w1, w2 = sb("w1", [RBF * G, 4, P]), sb("w2", [P, P])
        w3r, w3 = sb("w3r", [P, 2, C]), sb("w3", [P, 2, C])
        wl = sb("wl", [P, 2 * C])
        wsc = sb("wsc", [P, C])
        wagg, wv2 = sb("wagg", [P, 2, C + 1]), sb("wv2", [P, MUL])
        at_rows, cnt_rows = sb("at_rows", [NBLK, P]), sb("cnt_rows", [NBLK, 2, P])
        a_norm, a_in, a_agg = sb("a_norm", [P, NBLK]), sb("a_in", [P, NBLK]), sb("a_agg", [P, NBLK])
        xsum, xsq, eps = sb("xsum", [P, NBLK]), sb("xsq", [P, NBLK]), sb("eps", [P, 1])
        std, rstd, nmean = sb("std", [P, NBLK]), sb("rstd", [P, NBLK]), sb("nmean", [P, NBLK])
        base_i, tile0_i, off_i = sb("base_i", [ROWS, 1], I32), sb("tile0_i", [ROWS, 1], I32), sb("off_i", [ROWS, 1], I32)
        tile0_f, off_f, pad_off = sb("tile0_f", [ROWS, 1]), sb("off_f", [ROWS, 1]), sb("pad_off", [ROWS, 1])
        tot_i, grp_i = sb("tot_i", [P, 1], I32), sb("grp_i", [P, 1], I32)
        plan = sb("plan", [P, 3], I32)
        none = sb("none", [P, IDC])
        cnt_n, cmax, rcnt, scale = (sb(n, [P, NBLK]) for n in ("cnt_n", "cmax", "rcnt", "scale"))
        apre, alpha, salpha = sb("apre", [P, 2, BI]), sb("alpha", [P, 2, BI]), sb("salpha", [P, 2, BI])

        ps = ctx.enter_context(nc.psum_tensor("ps", [P, 8, 512], F32))
        unread = ps[:, 0:2, :].rearrange("p k (b c) -> p (k b) c", c=C)
        ps_hT = [ps[:, k, 0:C] for k in range(2)]
        ps_l = [ps[:, 2 + k, 0:2 * C] for k in range(4)]
        ps_a, ps_id = ps[:, 6, 0:NBLK], ps[:, 7, 0:IDC]
        ps_start, ps_total = ps[0:ROWS, 7, 0:1], ps[:, 7, 1:2]
        ps_w = [ps[:, 2 * s:2 * s + 2, :].rearrange("p k (t c) -> p (k t) c", c=C) for s in range(2)]
        ps_z, ps_x = ps[:, 4, :], ps[:, 5, :]
        ps_s = [ps[:, 6 + s, 0:FC * WIN].rearrange("p (c n) -> p c n", c=FC) for s in range(2)]
        def ps_e(s, j):
            return ps[:, 3 * s + j // 3, (j % 3) * (C + 1):(j % 3 + 1) * (C + 1)]

        s_x, s_at, s_dist, s_dst, s_src, s_attr = (sem(n) for n in ("x_in", "at_in", "dist_in", "dst_in", "src_in", "attr_in"))
        s_wraw, s_wz, s_tail, s_lfree = sem("weights_in"), sem("weights_zeroed"), sem("tails_zeroed"), sem("l_rows_stored")
        s_const, s_pool, s_dve, s_act = sem("consts"), sem("pool_step"), sem("dve_step"), sem("act_step")
        s_recp, s_reca, s_recd = sem("rec_src_dst"), sem("rec_dist_attr"), sem("rec_cnt")
        s_rtab, s_ltab = sem("rec_tab_written"), sem("l1_tab_written")
        s_mean, s_atT, s_ain, s_std, s_norm = (sem(n) for n in ("mean_ready", "attr_T", "attr_scaled", "std_ready", "norm_ready"))
        s_h, s_hTp, s_hT, s_lp, s_lsb, s_base, s_base_end = (sem(n) for n in ("h_ready", "hT_psum", "hT_ready", "l_psum", "l_ready", "base_ready", "base_end_ready"))
        s_wdone = sem("weights_ready")
        s_cnt, s_pre, s_off, s_ends, s_ebase = (sem(n) for n in ("row_counts", "row_starts", "rows_free", "ends_marked", "edge_base_ready"))
        s_ln, s_ide2, s_hotid, s_idp, s_ide, s_plan, s_ids = (sem(n) for n in ("ln_turn", "ids_none", "edge_no_ready", "ids_psum", "ids_psum_read", "plan_ready", "ids_ready"))
        s_gsh0, s_runs, s_sums, s_zero, s_hot16, s_settled = sem("first_harmonic_product"), sem("run_ends_ready"), sem("pool_sums"), sem("agg_zeroed"), sem("hot16_ready"), sem("sums_settled")
        s_idg, s_rc = sem("ids_g_ready"), sem("rec_copied")
        s_rec = [sem("rec_in0"), sem("rec_in1")]
        s_gat = [sem("gath_in0"), sem("gath_in1")]
        s_frac, s_sin, s_rbf, s_rT, s_rbfT = (sem(n) for n in ("frac_ready", "sin_ready", "rbf_ready", "rbfT_psum", "rbfT_ready"))
        s_z1, s_h1, s_z2, s_h2, s_w = (sem(n) for n in ("z1_ready", "h1_ready", "z2_ready", "h2_ready", "w_ready"))
        s_diag, s_bc, s_win = sem("diag_ready"), sem("windows_psum"), sem("windows_ready")
        s_far, s_pe, s_cut, s_msgc, s_ed, s_msg, s_hot, s_sum, s_add = (sem(n) for n in ("far_step_dve", "pe_step", "cut_steps", "msg_count_ready", "out_step", "msg_ready", "hot_ready", "sum_psum", "sum_added"))
        s_whot, s_wsum, s_wadd, s_wdve = (sem(n) for n in ("far_hot", "far_sum", "far_added", "far_step"))
        s_crow, s_cT, s_cn, s_ec, s_aggd, s_ab, s_eb, s_ap, s_al, s_fin, s_out = (sem(n) for n in ("cnt_rows_in", "cnt_T", "cnt_ready", "cnt_step", "agg_done", "aggb_ready", "out_psum", "alpha_pre", "alpha_ready", "out_ready", "out_written"))

        weight_loads = [(wl[0:MUL, 0:MUL], lin1_ws), (wsc[0:MUL, 0:MUL], sc_ws)]
        for m in range(3):
            weight_loads += [(wl[MUL + m:C:3, MUL + MUL * m:2 * MUL + MUL * m], lin1_wv),
                             (wsc[MUL + m:C:3, MUL + MUL * m:2 * MUL + MUL * m], sc_wv)]
        for t in range(G):
            weight_loads.append((w1[RBF * t:RBF * t + RBF, t // 2, HID * (t % 2):HID * (t % 2) + HID], fc_w1))
        for k in range(2):
            weight_loads += [(w2[HID * k:HID * k + HID, HID * k:HID * k + HID], fc_w2),
                             (w3r[HID * k:HID * k + HID, k, :], fc_w3),
                             (wv2[HID * k:HID * k + HID, :], lin2_wv)]
        weight_loads += [(wagg[0:2 * MUL, 0, 0:MUL], lin2_ws), (wagg[0:2 * MUL, 0, C:C + 1], alpha_w)]
        WZ = 6
        NCONST = 9 + 2 * RBF
        NWL = len(weight_loads)

        def edge_loop(engine, name, loops_n, turn, step):
            done = engine.alloc_register(name)
            engine.reg_mov(done, 0)
            for length in TURNS:
                with engine.If(loops_n - engine.snap(done) >= length):
                    first = engine.snap(done)
                    with engine.Fori(0, length) as k:
                        turn(first + k)
                    engine.reg_add(done, done, length)
                engine.sem_inc(step, 1)

        block = ctx.enter_context(nc.Block())

        @block.sync
        def _(sp):
            nlast = (NBLK - 1) * P
            for lo, hi in ((0, RA), (RA, ROWS)):
                sp.dma_start(work[lo:hi, CW:CW + LEN].bitcast(I32), dst.rearrange("(p e) -> p e", p=ROWS)[lo:hi, :]).then_inc(s_dst, 16)
                sp.dma_start(work[lo:hi, 0:LEN], edge_weight.rearrange("(p e) -> p e", p=ROWS)[lo:hi, :]).then_inc(s_dist, 16)
            sp.wait_ge(s_tail, 2)
            sp.dma_start(at_rows[0:NBLK - 1, :], node_vec1[0:nlast, :].rearrange("(b p) c -> b (p c)", p=P)).then_inc(s_at, 16)
            sp.dma_start(at_rows[NBLK - 1:NBLK, 0:TAIL], node_vec1[nlast:N, :].rearrange("(a p) c -> a (p c)", a=1)).then_inc(s_at, 16)
            sp.dma_start(base[:, 0:NBLK - 1, :], x[0:nlast, :].rearrange("(b p) c -> p b c", p=P)).then_inc(s_x, 16)
            sp.dma_start(base[0:TAIL, NBLK - 1, :], x[nlast:N, :]).then_inc(s_x, 16)
            for lo, hi in ((0, RA), (RA, ROWS)):
                sp.dma_start(work[lo:hi, 2 * CW:2 * CW + LEN].bitcast(I32), src.rearrange("(p e) -> p e", p=ROWS)[lo:hi, :]).then_inc(s_src, 16)
                sp.dma_start(big[lo:hi, (LEN + 1) * REC:(LEN + 1) * REC + 4 * LEN],
                             edge_attr_4.rearrange("(p e) f -> p (e f)", p=ROWS)[lo:hi, :]).then_inc(s_attr, 16)
            sp.wait_ge(s_wz, WZ)
            for n, (to, of) in enumerate(weight_loads):
                sp.dma_start(to, of).then_inc(s_wraw, 16)
            sp.wait_ge(s_recp, 3)
            sp.wait_ge(s_reca, 2)
            sp.wait_ge(s_recd, 1)
            tab = rec_tab[0:E, :].rearrange("(p e) f -> p (e f)", p=ROWS)
            for lo, hi in ((0, RA), (RA, ROWS)):
                sp.dma_start(tab[lo:hi, :], big[lo:hi, 0:LEN * REC]).then_inc(s_rtab, 16)
            sp.dma_start(rec_tab[E:E + 1, :], big[ROWS - 1:ROWS, LEN * REC:(LEN + 1) * REC]).then_inc(s_rtab, 16)
            l1_v = l1_tab.rearrange("(b p) c -> p b c", p=P)
            sp.sem_inc(s_lfree, 2)

            def store_lin1(i, s):
                sp.wait_ge(s_lsb, BI * i + BI + 1)
                sp.dma_start(l1_v[:, bass.ds(BI * i, BI), :], lsb[:, s, :, 0:C]).then_inc(s_ltab, 16)
                sp.wait_ge(s_ltab, 16 * i + 16)
                sp.sem_inc(s_lfree, 1)

            with sp.Fori(0, NI // 2) as j:
                store_lin1(2 * j, 0)
                store_lin1(2 * j + 1, 1)
            store_lin1(NI - 1, 0)
            sp.wait_ge(s_aggd, 1)
            for k in range(2):
                sp.dma_start(cnt_rows[:, k, :], agg[k:k + 1, 2, 0:NBLK * P].rearrange("a (b p) -> a b p", p=P)).then_inc(s_crow, 16)
            out_v = out[0:nlast, :].rearrange("(b p) c -> p b c", p=P)
            with sp.Fori(0, NI - 1) as i:
                sp.wait_ge(s_fin, i + 1)
                sp.dma_start(out_v[:, bass.ds(BI * i, BI), :], base[:, bass.ds(BI * i, BI), :]).then_inc(s_out, 16)
            sp.wait_ge(s_fin, NI)
            sp.dma_start(out_v[:, BI * (NI - 1):NBLK - 1, :], base[:, BI * (NI - 1):NBLK - 1, :]).then_inc(s_out, 16)
            sp.dma_start(out[nlast:N, :], base[0:TAIL, NBLK - 1, :]).then_inc(s_out, 16)
            sp.wait_ge(s_out, 16 * (NI + 1))

        @block.gpsimd
        def _(po):
            nc.gpsimd.memset(base[:, NBLK - 1, :], 0.0).then_inc(s_tail, 1)
            nc.gpsimd.iota(place1, pattern=[[1, LEN]], base=1, channel_multiplier=0,
                           allow_small_or_imprecise_dtypes=True).then_inc(s_const, 1)
            for m in (wl[:, :], wsc[:, :], w1[:, :, :], w2[:, :], w3r[:, :, :], wagg[:, :, :]):
                nc.gpsimd.memset(m, 0.0).then_inc(s_wz, 1)
            nc.gpsimd.memset(ones[:, :], 1.0).then_inc(s_const, 1)
            nc.gpsimd.memset(half_pi[:, :], pi / 2).then_inc(s_const, 1)
            nc.gpsimd.memset(eps[:, :], EPS).then_inc(s_const, 1)
            nc.gpsimd.memset(move, 0).then_inc(s_const, 1)
            nc.gpsimd.memset(cnt16[:, :, :], 0.0).then_inc(s_const, 1)
            nc.gpsimd.memset(ident[:, :], 0.0).then_inc(s_pool, 1)
            nc.gpsimd.memset(tri[:, :], 1.0).then_inc(s_pool, 1)
            po.wait_ge(s_pool, 2)
            nc.gpsimd.affine_select(out=ident[:, :], in_=ident[:, :], compare_op=ALU.not_equal, fill=1.0,
                                    base=0, pattern=[[-1, P]], channel_multiplier=1).then_inc(s_const, 1)
            nc.gpsimd.affine_select(out=tri[:, :], in_=tri[:, :], compare_op=ALU.is_gt, fill=0.0,
                                    base=0, pattern=[[1, P]], channel_multiplier=-1).then_inc(s_const, 1)
            nc.gpsimd.iota(iota[:, :], pattern=[[1, WIN]], base=0, channel_multiplier=0,
                           allow_small_or_imprecise_dtypes=True).then_inc(s_const, 1)
            for k in range(RBF):
                nc.gpsimd.memset(kturn[:, k:k + 1], (k + 1) / (2 * CUTOFF)).then_inc(s_const, 1)
                nc.gpsimd.memset(kfreq[:, k:k + 1], (k + 1) * pi / CUTOFF).then_inc(s_const, 1)
            po.wait_ge(s_x, 32)
            terms, width = base[:, 0:BI * NI_P, :], C
            while width > 1:
                width //= 2
                sums = part_sums[:, :, 0:width] if width > 1 else xsum[:, 0:BI * NI_P].unsqueeze(2)
                nc.gpsimd.tensor_tensor(sums, terms[:, :, 0:width], terms[:, :, width:2 * width], ALU.add).then_inc(s_sums, 1)
                po.wait_ge(s_sums, SUM_STEPS - width.bit_length() + 1)
                terms = sums
            po.wait_ge(s_src, 32)
            nc.gpsimd.tensor_copy(rec_rows[:, 0:LEN, SRC:SRC + 1].rearrange("p e f -> p (e f)"), src_raw.bitcast(I32)).then_inc(s_recp, 1)
            po.wait_ge(s_ends, 1)
            nc.gpsimd.tensor_copy(rec_rows[:, 0:LEN, DST:DST + 1].rearrange("p e f -> p (e f)"), dst_f[:, 0:LEN]).then_inc(s_recp, 1)
            po.wait_ge(s_runs, 1)
            nc.gpsimd.tensor_tensor(rec_rows[:, 0:LEN, CNT:CNT + 1].rearrange("p e f -> p (e f)"), run_end, run_start[:, 0:LEN],
                                    ALU.subtract).then_inc(s_recp, 1)
            po.wait_ge(s_recp, 1)
            nc.gpsimd.iota(edge_base, pattern=[[1, W]], base=1 - PAD, channel_multiplier=LEN,
                           allow_small_or_imprecise_dtypes=True).then_inc(s_ebase, 1)
            po.wait_ge(s_recp, 3)
            po.wait_ge(s_off, 1)
            nc.gpsimd.iota(tile_no, pattern=[[1, P // 8 + IDW]], base=-(P // 8), channel_multiplier=0,
                           allow_small_or_imprecise_dtypes=True).then_inc(s_ebase, 1)
            po.sem_inc(s_base, 2)
            po.sem_inc(s_hTp, BI + 1)
            po.wait_ge(s_mean, 1)
            po.wait_ge(s_reca, 2)

            def add_self(i, s):
                po.wait_ge(s_lsb, BI * i + BI + 1)
                nc.gpsimd.tensor_tensor(base[:, bass.ds(BI * i, BI), :], base[:, bass.ds(BI * i, BI), :],
                                        lsb[:, s, :, C:2 * C], ALU.add).then_inc(s_base, 1)

            def centre(i, s):
                po.wait_ge(s_hTp, BI * i + 1)
                po.sem_inc(s_pool)
                nc.gpsimd.tensor_tensor(centred[:, s, :, :], base[:, bass.ds(BI * i, BI), :],
                                        nmean[:, bass.ds(BI * i, BI)].unsqueeze(2).broadcast_to([P, BI, C]), ALU.add).then_inc(s_h, 1)

            centre(0, 0)
            centre(1, 1)
            with po.Fori(0, NI_A // 2) as j:
                centre(2 * j + 2, 0)
                add_self(2 * j, 0)
                centre(2 * j + 3, 1)
                add_self(2 * j + 1, 1)
            for i in range(NI_A // 2 * 2, NI_A):
                centre(i + 2, i % 2)
                add_self(i, i % 2)

            def gather_records(s):
                for t in range(G):
                    po.indirect_dma_start(rec[:, s, t, :], None, rec_tab,
                                          bass.IndirectOffsetOnAxis(ids_g[:, s, t:t + 1], 0)).then_inc(s_rec[s], 16)

            def gather_sources(s):
                for t in range(G):
                    po.indirect_dma_start(gath[:, s, t, :], None, l1_tab,
                                          bass.IndirectOffsetOnAxis(src_g[:, s, t:t + 1], 0)).then_inc(s_gat[s], 16)

            po.wait_ge(s_rtab, 48)
            po.wait_ge(s_plan, 1)
            groups_n = po.value_load(plan[0:1, 0:1], min_val=2, max_val=GROUPS)
            loops_n = po.value_load(plan[0:1, 1:2], min_val=0, max_val=GROUPS // 2)
            odd = po.value_load(plan[0:1, 2:3], min_val=0, max_val=1)
            po.wait_ge(s_idg, 1)
            gather_records(0)
            po.wait_ge(s_idg, 2)
            gather_records(1)
            po.wait_ge(s_ltab, 16 * NI)

            def half(i, s, ahead=True):
                g = 2 * i + s
                po.wait_ge(s_rc, g + 2)
                po.sem_inc(s_pool)
                po.wait_ge(s_msg, g + 1)
                po.sem_inc(s_pool)
                gather_sources(s)
                if ahead:
                    po.wait_ge(s_idg, g + 3)
                    po.sem_inc(s_pool)
                    gather_records(s)

            def turn(i):
                half(i, 0)
                half(i, 1)

            edge_loop(po, "turns_po", loops_n, turn, s_pool)
            with po.If(odd > 0):
                half(loops_n, 0)
                half(loops_n, 1, ahead=False)
                half(loops_n + 1, 0, ahead=False)
            po.sem_inc(s_pool)
            with po.If(odd < 1):
                half(loops_n, 0, ahead=False)
                half(loops_n, 1, ahead=False)
            po.sem_inc(s_pool)

        @block.scalar
        def _(act):
            act.wait_ge(s_dist, 32)
            nc.scalar.activation(rec_rows[:, 0:LEN, 0:1].rearrange("p e f -> p (e f)"), dist, ACT.Copy).then_inc(s_reca, 1)
            act.wait_ge(s_x, 32)
            act.wait_ge(s_const, NCONST)
            act.sem_inc(s_ln, 1)
            with act.Fori(0, NI - NI_P) as i:
                act.wait_ge(s_ln, BI * i + 1)
                act.sem_inc(s_act, 1)
                for j in range(BI):
                    b = BI * (i + NI_P) + j
                    nc.scalar.activation(unread[:, j, :], base[:, bass.ds(b, 1), :].rearrange("p a c -> p (a c)"), ACT.Copy,
                                         accum_out=xsum[:, bass.ds(b, 1)]).then_inc(s_ln, 1)
            act.wait_ge(s_ln, BI * (NI - NI_P) + 1)
            act.wait_ge(s_sums, SUM_STEPS)
            nc.scalar.activation(nmean[:, :], xsum[:, :], ACT.Copy, scale=-1.0 / C).then_inc(s_mean, 1)
            act.wait_ge(s_attr, 32)
            nc.scalar.activation(rec_rows[:, 0:LEN, SH:SH + 4], attr_rows.rearrange("p (e f) -> p e f", f=4), ACT.Copy).then_inc(s_reca, 1)
            act.wait_ge(s_mean, 1)
            with act.Fori(0, NI) as i:
                act.wait_ge(s_ln, BI * (NI - NI_P) + BI * i + 1)
                act.sem_inc(s_act, 1)
                for j in range(BI):
                    b = BI * i + j
                    nc.scalar.activation(unread[:, j, :], base[:, bass.ds(b, 1), :].rearrange("p a c -> p (a c)"), ACT.Square,
                                         bias=nmean[:, bass.ds(b, 1)], accum_out=xsq[:, bass.ds(b, 1)]).then_inc(s_ln, 1)
            act.wait_ge(s_ln, BI * (NI - NI_P) + NBLK + 1)
            nc.scalar.activation(std[:, :], xsq[:, :], ACT.Sqrt, scale=1.0 / C, bias=eps[:, 0:1]).then_inc(s_std, 1)
            act.wait_ge(s_atT, 1)
            nc.scalar.activation(a_in[:, :], ps_a, ACT.Copy, scale=1.0 / sqrt(MUL)).then_inc(s_ain, 1)
            nc.scalar.activation(a_agg[:, :], ps_a, ACT.Copy, scale=1.0 / sqrt(2 * MUL)).then_inc(s_ain, 1)
            act.wait_ge(s_wraw, 16 * NWL)
            nc.scalar.activation(wl[:, C:C + MUL], wsc[:, 0:MUL], ACT.Copy).then_inc(s_wdone, 1)
            nc.scalar.activation(wl[:, C + MUL:2 * C].rearrange("p (o m) -> p m o", m=3),
                                 wsc[:, MUL:C].rearrange("p (m o) -> p m o", m=3), ACT.Copy).then_inc(s_wdone, 1)
            for m in range(3):
                k = m + 1
                rows = slice(HID * (k % 2), HID * (k % 2) + HID)
                nc.scalar.activation(wagg[rows, k // 2, MUL:C].rearrange("p (o m) -> p m o", m=3)[:, m, :],
                                     wv2[rows, :], ACT.Copy).then_inc(s_wdone, 1)
            act.wait_ge(s_norm, 1)
            act.wait_ge(s_reca, 2)
            act.wait_ge(s_ain, 2)
            act.sem_inc(s_hT, 1)
            act.sem_inc(s_lsb, 1)
            def lin1(i, s):
                for j in range(1, BI + 2):
                    if j <= BI:
                        act.wait_ge(s_hTp, BI * i + j + BI + 1)
                        nc.scalar.activation(hT[:, j - 1, :], ps_hT[(j - 1) % 2], ACT.Relu).then_inc(s_hT, 1)
                    if j >= 2:
                        act.wait_ge(s_lp, BI * i + j - 1)
                        if j == 2:
                            act.wait_ge(s_lfree, i + 1)
                            act.wait_ge(s_base, i + 1)
                        nc.scalar.activation(lsb[:, s, j - 2, :], ps_l[(j - 2) % 4], ACT.Copy,
                                             scale=a_norm[:, bass.ds(BI * i + j - 2, 1)]).then_inc(s_lsb, 1)

            with act.Fori(0, NI_A // 2) as j:
                lin1(2 * j, 0)
                lin1(2 * j + 1, 1)
            for i in range(NI_A // 2 * 2, NI_A):
                lin1(i, i % 2)

            def edge_numbers(g, s):
                nc.scalar.activation(ids_g[:, s, :], ids[:, bass.ds(G * g, G)], ACT.Copy).then_inc(s_idg, 1)

            act.wait_ge(s_ide, 1)
            nc.scalar.activation(ids_g[:, 0, :], ids[:, 0:G], ACT.Copy).then_inc(s_idg, 1)
            nc.scalar.activation(ids_g[:, 1, :], ids[:, G:2 * G], ACT.Copy).then_inc(s_idg, 1)
            for i in range(NI_A, NI):
                lin1(i, i % 2)
            def times_first(g, s, i):
                act.wait_ge(s_gat[s], GIN * i + GIN)
                act.sem_inc(s_act, 1)
                act.wait_ge(s_msg, g + 2)
                for t in range(G):
                    ins = nc.scalar.activation(gsh0[:, t, :], gath[:, s, t, :], ACT.Copy, scale=recw[:, s, t, SH:SH + 1])
                ins.then_inc(s_gsh0, 1)

            act.wait_ge(s_plan, 1)
            loops_n = act.value_load(plan[0:1, 1:2], min_val=0, max_val=GROUPS // 2)
            odd = act.value_load(plan[0:1, 2:3], min_val=0, max_val=1)
            def mlp(g):
                act.wait_ge(s_frac, g + 1)
                nc.scalar.activation(sinv[:, :, :], frac[:, :, :], ACT.Sin, scale=2 * pi)
                nc.scalar.activation(cosv[:, :], d6[:, :], ACT.Sin, scale=-pi / (2 * CUTOFF), bias=half_pi[:, 0:1]).then_inc(s_sin, 1)
                act.wait_ge(s_rT, g + 1)
                nc.scalar.activation(rbfT[:, :], ps_z[0:RBF * G, 0:P], ACT.Copy).then_inc(s_rbfT, 1)
                act.wait_ge(s_z1, g + 1)
                nc.scalar.activation(h1[:, :], ps_z, ACT.Silu, scale=1.0 / sqrt(RBF)).then_inc(s_h1, 1)
                act.wait_ge(s_z2, g + 1)
                nc.scalar.activation(h2[:, :], ps_z, ACT.Silu, scale=1.0 / sqrt(HID)).then_inc(s_h2, 1)

            def next_numbers(g, s, i):
                act.wait_ge(s_rec[s], GIN * i + GIN)
                edge_numbers(g + 2, s)

            def hot_copy(g, s):
                act.wait_ge(s_hot, g + 1)
                nc.scalar.activation(hot16[:, :, :], hot[:, s, :, :], ACT.Copy).then_inc(s_hot16, 1)

            for s in range(2):
                next_numbers(s, s, 0)
                mlp(s)
            hot_copy(0, 0)
            act.wait_ge(s_ids, 1)
            times_first(0, 0, 0)

            def half(i, s, ahead=True, following=True, settled=0):
                g = 2 * i + s
                if ahead:
                    next_numbers(g + 2, s, i + 1)
                    mlp(g + 2)
                elif following:
                    act.wait_ge(s_settled, settled)
                if following:
                    times_first(g + 1, 1 - s, i + s)
                    hot_copy(g + 1, 1 - s)

            def turn(i):
                half(i, 0)
                half(i, 1)

            edge_loop(act, "turns_act", loops_n, turn, s_act)
            with act.If(odd > 0):
                half(loops_n, 0)
                half(loops_n, 1, ahead=False, settled=1)
            act.sem_inc(s_act, 1)
            with act.If(odd < 1):
                half(loops_n, 0, ahead=False, settled=1)
            act.sem_inc(s_act, 1)

            act.wait_ge(s_aggd, 1)

            def sums_out(i, s, first):
                if not first:
                    act.wait_ge(s_eb, i - 1)
                nc.scalar.activation(aggb[s], agg[:, 0:2, bass.ds(BI * P * i, BI * P)], ACT.Copy).then_inc(s_ab, 1)

            def gate(i, s):
                act.wait_ge(s_ap, i + 1)
                nc.scalar.activation(alpha[:, s, :], apre[:, s, :], ACT.Tanh).then_inc(s_al, 1)

            sums_out(0, 0, True)
            act.wait_ge(s_cT, 1)
            nc.scalar.activation(cnt_n[:, :], ps_a, ACT.Copy).then_inc(s_cn, 1)
            sums_out(1, 1, True)
            gate(0, 0)
            sums_out(2, 0, False)
            with act.Fori(0, (NI - 3) // 2) as i:
                for s in range(2):
                    gate(2 * i + 1 + s, 1 - s)
                    sums_out(2 * i + 3 + s, 1 - s, False)
            gate(NI - 2, 1)
            gate(NI - 1, 0)

        @block.vector
        def _(dve):
            v = nc.vector
            step = [0]

            def did(ins):
                step[0] += 1
                ins.then_inc(s_dve, 1)
                return step[0]

            def link(ins):
                dve.wait_ge(s_dve, did(ins))

            v.memset(at_rows[:, :], 0.0).then_inc(s_tail, 1)
            dve.wait_ge(s_dst, 32)
            did(v.tensor_copy(dst_f[:, 0:LEN], dst_raw.bitcast(I32)))
            did(v.memset(dst_f[:, LEN:LEN + 1], -1.0))
            did(v.memset(run_start[:, 0:1], 0.0))
            did(v.memset(listed[:, LEN:LEN + 1], 0.0))
            dve.wait_ge(s_dve, step[0])
            v.tensor_tensor(listed[:, 0:LEN], dst_f[:, 0:LEN], dst_f[:, 1:LEN + 1], ALU.not_equal).then_inc(s_ends, 1)
            dve.wait_ge(s_ends, 1)
            dve.wait_ge(s_const, NCONST)
            link(v.tensor_tensor(end_mark, listed[:, 0:LEN], place1, ALU.mult))
            link(v.tensor_tensor_scan(out=run_start[:, 1:LEN + 1], data0=end_mark, data1=end_mark, initial=0.0, op0=ALU.max, op1=ALU.max))
            dve.wait_ge(s_dist, 32)
            dve.wait_ge(s_reca, 1)
            link(v.scalar_tensor_tensor(out=near, in0=dist, scalar=CUTOFF, in1=place1, op0=ALU.is_le, op1=ALU.mult))
            did(v.tensor_tensor_scan(out=near_last, data0=near, data1=near, initial=0.0, op0=ALU.max, op1=ALU.max))
            link(v.scalar_tensor_tensor(out=temp[:, 0:LEN], in0=run_start[:, 0:LEN], scalar=1.0, in1=listed[:, 0:LEN], op0=ALU.add, op1=ALU.mult))
            link(v.tensor_tensor(listed[:, 0:LEN], temp[:, 0:LEN], near_last, ALU.is_gt))
            link(v.scalar_tensor_tensor(out=listed[:, 0:LEN], in0=near, scalar=0.0, in1=listed[:, 0:LEN], op0=ALU.is_gt, op1=ALU.max))
            link(v.tensor_scalar(temp, listed, -1.0, 1.0, ALU.mult, ALU.add))
            v.tensor_tensor_scan(out=run_end[:, ::-1], data0=temp[:, 1:LEN + 1][:, ::-1], data1=end_mark[:, ::-1],
                                 initial=0.0, op0=ALU.mult, op1=ALU.add).then_inc(s_runs, 1)
            dve.wait_ge(s_runs, 1)
            link(v.tensor_tensor_scan(out=rank, data0=listed[:, 0:LEN], data1=listed[:, 0:LEN], initial=0.0, op0=ALU.add, op1=ALU.max))
            v.tensor_copy(tile0_f[:, :], rank[:, LEN - 1:LEN]).then_inc(s_cnt, 1)
            link(v.memset(rec_rows[:, LEN, :], 0.0))
            did(v.memset(rec_rows[:, LEN, 0:1], 8 * CUTOFF))
            v.tensor_copy(rec_rows[:, LEN, DST:DST + 1], dst_f[:, LEN - 1:LEN]).then_inc(s_recd, 1)

            dve.wait_ge(s_pre, 1)
            link(v.tensor_copy(base_i[:, :], ps_start))
            did(v.tensor_single_scalar(tile0_i[:, :], base_i[:, :], 7, ALU.logical_shift_right))
            did(v.tensor_single_scalar(off_i[:, :], base_i[:, :], P - 1, ALU.bitwise_and))
            link(v.tensor_scalar(tot_i[:, :], ps_total, float(G * P - 1), None, ALU.add))
            did(v.tensor_copy(tile0_f[:, :], tile0_i[:, :]))
            link(v.tensor_copy(off_f[:, :], off_i[:, :]))
            did(v.tensor_scalar(pad_off[:, :], off_f[:, :], -1.0, float(PAD), ALU.mult, ALU.add))
            link(v.tensor_tensor(shift0, place1, rank, ALU.subtract))
            did(v.memset(sh_a[:, 0:PAD], 0))
            did(v.memset(sh_a[:, PAD + LEN:W], 0))
            dve.wait_ge(s_dve, step[0])
            v.scalar_tensor_tensor(out=sh_a[:, PAD:PAD + LEN], in0=shift0, scalar=pad_off[:, 0:1], in1=listed[:, 0:LEN],
                                   op0=ALU.add, op1=ALU.mult).then_inc(s_off, 1)
            dve.wait_ge(s_off, 1)

            now, new = sh_a, sh_b
            for k in range(STEPS):
                if k == 5:
                    dve.wait_ge(s_std, 1)
                    dve.wait_ge(s_ain, 2)
                    link(v.reciprocal(rstd[:, :], std[:, :]))
                    v.tensor_tensor(a_norm[:, :], a_in[:, :], rstd[:, :], ALU.mult).then_inc(s_norm, 1)
                link(v.tensor_scalar(stay, now, k, 1, ALU.logical_shift_right, ALU.bitwise_and))
                link(v.tensor_tensor(move[:, 0:W], stay, now, ALU.mult))
                link(v.tensor_tensor(stay, now, move[:, 0:W], ALU.subtract))
                link(v.tensor_tensor(new, stay, move[:, 2 ** k:2 ** k + W], ALU.add))
                now, new = new, now

            dve.wait_ge(s_ebase, 2)
            dve.wait_ge(s_recp, 2)
            n = did(v.scalar_tensor_tensor(out=edge_no, in0=now, scalar=0.0, in1=edge_base, op0=ALU.is_gt, op1=ALU.mult))
            link(v.tensor_scalar(tile_hot, tile_no, tile0_f[:, 0:1], None, ALU.is_equal))
            v.tensor_tensor(edge_no, edge_no, now, ALU.add).then_inc(s_hotid, 1)
            link(v.tensor_single_scalar(grp_i[:, :], tot_i[:, :], 10, ALU.logical_shift_right))
            link(v.tensor_scalar(plan[:, 0:1], grp_i[:, :], 2, None, ALU.max))
            did(v.tensor_single_scalar(plan[:, 2:3], plan[:, 0:1], 1, ALU.bitwise_and))
            link(v.tensor_scalar(grp_i[:, :], plan[:, 0:1], 2, None, ALU.subtract))
            v.tensor_single_scalar(plan[:, 1:2], grp_i[:, :], 1, ALU.logical_shift_right).then_inc(s_plan, 1)
            dve.wait_ge(s_wraw, 16 * NWL)
            did(v.tensor_scalar(w3[:, :, 0:3 * MUL], w3r[:, :, 0:3 * MUL], 1.0 / sqrt(HID), None, ALU.mult))
            did(v.tensor_scalar(w3[:, :, 3 * MUL:C], w3r[:, :, 3 * MUL:C], 1.0 / sqrt(HID) / sqrt(3.0), None, ALU.mult))
            dve.wait_ge(s_plan, 1)
            groups_n = dve.value_load(plan[0:1, 0:1], min_val=2, max_val=GROUPS)
            loops_n = dve.value_load(plan[0:1, 1:2], min_val=0, max_val=GROUPS // 2)
            odd = dve.value_load(plan[0:1, 2:3], min_val=0, max_val=1)

            def zero(c):
                if c == 0:
                    dve.wait_ge(s_rtab, 48)
                if c == 2:
                    dve.wait_ge(s_ltab, 16 * NI)
                    dve.wait_ge(s_base, NI_A + 2)
                v.memset(agg[:, c, :], 0.0).then_inc(s_zero, 1)

            def ids_out(c):
                first, tiles = IDS[c]
                dve.wait_ge(s_idp, c + 1)
                v.tensor_scalar(none[:, 0:tiles], ps_id[:, 0:tiles], 0.0, float(E + 1), ALU.is_equal, ALU.mult).then_inc(s_ide2, 1)
                dve.wait_ge(s_ide2, c + 1)
                v.scalar_tensor_tensor(out=ids[:, first:first + tiles], in0=ps_id[:, 0:tiles], scalar=-1.0, in1=none[:, 0:tiles],
                                       op0=ALU.add, op1=ALU.add).then_inc(s_ide, 1)
                dve.wait_ge(s_ide, c + 1)

            def add_self(i):
                dve.wait_ge(s_lsb, BI * i + BI + 1)
                x_in = base[:, BI * i:BI * (i + 1), :]
                v.tensor_tensor(x_in, x_in, lsb[:, i % 2, :, C:2 * C], ALU.add).then_inc(s_base_end, 1)

            ids_out(0)
            zero(0)
            zero(1)

            sh = [recw[:, s, :, SH:SH + 4] for s in range(2)]
            PER = 24
            before = step[0]

            class Steps:
                def __init__(self, start):
                    self.start, self.n = start, 0

                def did(self, ins):
                    self.n += 1
                    ins.then_inc(s_dve, 1)
                    return self.n

                def need(self, n):
                    dve.wait_ge(s_dve, self.start + n)

            one64 = ones[:, 0:G * RBF].rearrange("p (t k) -> p t k", t=G)

            def radial(g, s, i, own, first=False):
                dve.wait_ge(s_rec[s], GIN * i + GIN)
                own.did(v.tensor_copy(recw[:, s, :, :], rec[:, s, :, :]))
                a = own.did(v.tensor_scalar(d6[:, :], rec[:, s, :, 0], CUTOFF, None, ALU.min))
                v.tensor_copy(src_g[:, s, :], rec[:, s, :, SRC]).then_inc(s_rc, 1)
                own.need(a)
                dm = d6[:, :].unsqueeze(2).broadcast_to([P, G, RBF])
                a = own.did(v.tensor_tensor(turns[:, :, :], dm, kturn[:, :].unsqueeze(1).broadcast_to([P, G, RBF]), ALU.mult))
                b = own.did(v.tensor_tensor(fd[:, :, :], dm, kfreq[:, :].unsqueeze(1).broadcast_to([P, G, RBF]), ALU.mult))
                own.need(a)
                a = own.did(v.tensor_scalar(whole[:, :, :], turns[:, :, :], ROUND, ROUND, ALU.add, ALU.subtract))
                own.need(b)
                b = own.did(v.scalar_tensor_tensor(out=rfd[:, :, :], in0=fd[:, :, :], scalar=-1.0, in1=fd[:, :, :], op0=ALU.mult, op1=ALU.max))
                own.need(b)
                own.did(v.tensor_scalar(small[:, :, :], rfd[:, :, :], SMALL, None, ALU.is_lt))
                own.need(own.n)
                v.tensor_tensor(frac[:, :, :], turns[:, :, :], whole[:, :, :], ALU.subtract).then_inc(s_frac, 1)
                own.did(v.copy_predicated(fd[:, :, :], small[:, :, :], one64))
                if not first:
                    dve.wait_ge(s_rT, g)
                own.did(v.tensor_copy(dst_c[:, :], recw[:, s, :, DST]))

            def basis(g, s, own):
                own.need(own.n)
                a = own.did(v.reciprocal(rfd[:, :, :], fd[:, :, :]))
                dve.wait_ge(s_sin, g + 1)
                own.need(a)
                a = own.did(v.tensor_tensor(cut2[:, :], cosv[:, :], cosv[:, :], ALU.mult))
                b = own.did(v.tensor_tensor(rb[:, :, :], sinv[:, :, :], rfd[:, :, :], ALU.mult))
                own.need(b)
                v.scalar_tensor_tensor(out=cut[:, :], in0=recw[:, s, :, 0], scalar=CUTOFF, in1=cut2[:, :],
                                       op0=ALU.is_le, op1=ALU.mult).then_inc(s_cut, 1)
                v.copy_predicated(rb[:, :, :], small[:, :, :], one64).then_inc(s_cut, 1)
                dve.wait_ge(s_cut, 2 * g + 2)
                v.tensor_tensor(rbf[:, :].rearrange("p (t k) -> p t k", t=G), rb[:, :, :],
                                cut[:, :].unsqueeze(2).broadcast_to([P, G, RBF]), ALU.mult).then_inc(s_rbf, 1)

            def extent(g, own):
                dve.wait_ge(s_rT, g + 1)
                own.did(v.tensor_reduce(minmax[:, 0:1], ps_x[0:G, P:2 * P], AX_X, ALU.min))
                a = own.did(v.tensor_reduce(minmax[:, 1:2], ps_x[0:G, P:2 * P], AX_X, ALU.max))
                own.need(a)
                v.tensor_tensor(diag[:, :, :], ident[0:G, 0:G].unsqueeze(1).broadcast_to([G, 2, G]),
                                minmax[:, :].unsqueeze(2).broadcast_to([G, 2, G]), ALU.mult).then_inc(s_diag, 1)

            def windows(g, s, own):
                dve.wait_ge(s_bc, g + 1)
                lows = ps_x[:, 2 * P:2 * P + G].rearrange("p (q t) -> p q t", t=2)
                highs = ps_x[:, 2 * P + G:2 * P + 2 * G].rearrange("p (q t) -> p q t", t=2)
                own.did(v.tensor_reduce(win0[:, :], lows, AX_X, ALU.min))
                a = own.did(v.tensor_reduce(winmax[:, :], highs, AX_X, ALU.max))
                own.need(a)
                a = own.did(v.tensor_tensor(span4[:, :], winmax[:, :], win0[:, :], ALU.subtract))
                v.tensor_copy(win0_i[:, s, :], win0[:, :]).then_inc(s_win, 1)
                v.tensor_tensor(dloc[:, s, :].rearrange("p (q t) -> p q t", t=2),
                                recw[:, s, :, DST].rearrange("p (q t) -> p q t", t=2),
                                win0[:, :].unsqueeze(2).broadcast_to([P, NPAIR, 2]), ALU.subtract).then_inc(s_win, 1)
                own.need(a)
                v.tensor_reduce(span_i[:, s:s + 1], span4[:, :], AX_X, ALU.max).then_inc(s_win, 1)

            def messages(g, s, i, own):
                gs, gv = gath[:, s, :, 0:MUL], gath[:, s, :, MUL:C].rearrange("p t (m c) -> p t m c", m=3)
                w = ps_w[s]
                shm = sh[s][:, :, 1:4].unsqueeze(3).broadcast_to([P, G, 3, MUL])
                dve.wait_ge(s_gat[s], GIN * i + GIN)
                tv = own.did(v.tensor_tensor(gsh1[:, :, :, :], gv, shm, ALU.mult))
                dve.wait_ge(s_w, g + 1)
                tt = own.did(v.tensor_tensor(t01[:, :, :], gs, w[:, :, MUL:2 * MUL], ALU.mult))
                own.need(tv)
                d1 = own.did(v.tensor_tensor(dot1[:, :, :], gsh1[:, :, 0, :], gsh1[:, :, 1, :], ALU.add))
                own.need(d1)
                d2 = own.did(v.tensor_tensor(dot2[:, :, :], dot1[:, :, :], gsh1[:, :, 2, :], ALU.add))
                mv_ = msg[:, :, 2 * MUL:2 * C].rearrange("p t (m k c) -> p t m k c", m=3, k=2)
                own.need(d2)
                own.did(v.tensor_tensor(msg[:, :, MUL:2 * MUL], dot2[:, :, :], w[:, :, 3 * MUL:C], ALU.mult))
                own.did(v.tensor_tensor(mv_[:, :, :, 0, :], t01[:, :, :].unsqueeze(2).broadcast_to([P, G, 3, MUL]), shm, ALU.mult))
                dve.wait_ge(s_gsh0, g + 1)
                own.did(v.tensor_tensor(msg[:, :, 0:MUL], gsh0[:, :, 0:MUL], w[:, :, 0:MUL], ALU.mult))
                v.tensor_tensor(mv_[:, :, :, 1, :], gsh0[:, :, MUL:C].rearrange("p t (m c) -> p t m c", m=3),
                                w[:, :, 2 * MUL:3 * MUL].unsqueeze(2).broadcast_to([P, G, 3, MUL]), ALU.mult).then_inc(s_msg, 1)
                v.tensor_scalar(cnt16[:, :, 0], recw[:, s, :, CNT], 0.0, None, ALU.max).then_inc(s_msgc, 1)
                dve.wait_ge(s_msgc, 2 * g + 1)
                v.scalar_tensor_tensor(out=cnt16[:, :, 1], in0=recw[:, s, :, CNT], scalar=0.0, in1=cnt16[:, :, 0],
                                       op0=ALU.max, op1=ALU.subtract).then_inc(s_msgc, 1)

            def one_hot(s):
                return v.tensor_tensor(hot[:, s, :, :], iota[:, :].unsqueeze(1).broadcast_to([P, G, WIN]),
                                       dloc[:, s, :].unsqueeze(2).broadcast_to([P, G, WIN]), ALU.is_equal)

            def add_window(q, start):
                part = agg[:, :, bass.ds(start, WIN)]
                return v.tensor_tensor(part, part, ps_s[q % 2], ALU.add)

            far_turns = dve.alloc_register("far_turns_dve")
            dve.reg_mov(far_turns, 0)

            def far_windows(g, s, span):
                dve.wait_ge(s_add, NPAIR * g + NPAIR + 2)
                dve.sem_inc(s_far, 1)
                with dve.Fori(1, FAR) as k:
                    with dve.If(span >= WIN * k):
                        turn = dve.snap(far_turns)
                        dve.wait_ge(s_whot, turn + 1)
                        v.tensor_scalar(dloc[:, s, :], dloc[:, s, :], float(WIN), None, ALU.subtract).then_inc(s_wdve, 1)
                        v.tensor_scalar(win0_i[:, s, :], win0_i[:, s, :], WIN, NBLK * P, ALU.add, ALU.min).then_inc(s_wdve, 1)
                        dve.wait_ge(s_wdve, 3 * turn + 2)
                        one_hot(s).then_inc(s_wdve, 1)
                        dve.wait_ge(s_wdve, 3 * turn + 3)
                        v.tensor_copy(hot16[:, :, :], hot[:, s, :, :]).then_inc(s_whot, 1)
                        for q in range(NPAIR):
                            start = dve.value_load(win0_i[0:1, s, q:q + 1], min_val=0, max_val=NBLK * P)
                            dve.wait_ge(s_wsum, NPAIR * turn + q + 1)
                            dve.wait_ge(s_wadd, NPAIR * turn + q + 1)
                            add_window(q, start).then_inc(s_wadd, 1)
                        dve.reg_add(far_turns, far_turns, 1)
                dve.wait_ge(s_wadd, NPAIR * dve.snap(far_turns) + 1)
                dve.sem_inc(s_far, 1)

            def one_hot_of(g, s):
                dve.wait_ge(s_win, 3 * g + 3)
                one_hot(s).then_inc(s_hot, 1)

            def add_sum(g, s, q, start):
                dve.wait_ge(s_sum, NPAIR * g + q + 1)
                dve.wait_ge(s_add, NPAIR * g + q + 2)
                add_window(q, start).then_inc(s_add, 1)

            own = Steps(before)
            dve.sem_inc(s_rc, 1)
            dve.sem_inc(s_msg, 2)
            dve.sem_inc(s_add, 2)
            dve.sem_inc(s_whot, 1)
            dve.sem_inc(s_wadd, 1)

            radial(0, 0, 0, own, first=True)
            basis(0, 0, own)
            for i in range(NI_A, NI):
                add_self(i)
            for c in range(1, len(IDS)):
                with dve.If(groups_n > IDS[c][0] // G - 4):
                    ids_out(c)
            dve.sem_inc(s_ids, 1)
            extent(0, own)
            zero(2)
            windows(0, 0, own)
            one_hot_of(0, 0)
            radial(1, 1, 0, own)
            basis(1, 1, own)
            dve.wait_ge(s_zero, 3)
            start0 = before + own.n

            def half(i, s, own, ahead=True, following=True):
                g = 2 * i + s
                if following:
                    extent(g + 1, own)
                messages(g, s, i, own)
                if following:
                    windows(g + 1, 1 - s, own)
                    one_hot_of(g + 1, 1 - s)
                start = [dve.value_load(win0_i[0:1, s, q:q + 1], min_val=0, max_val=N - 1) for q in range(NPAIR)]
                add_sum(g, s, 0, start[0])
                if ahead:
                    radial(g + 2, s, i + 1, own)
                add_sum(g, s, 1, start[1])
                if ahead:
                    basis(g + 2, s, own)
                add_sum(g, s, 2, start[2])
                add_sum(g, s, 3, start[3])
                span = dve.value_load(span_i[0:1, s:s + 1], min_val=0, max_val=N)
                with dve.If(span >= WIN):
                    far_windows(g, s, span)
                dve.sem_inc(s_far, 1)

            def turn(i):
                for s in range(2):
                    own = Steps(i * (2 * PER) + (start0 + s * PER))
                    half(i, s, own)
                    assert own.n == PER, own.n

            def last_half(i, s, own, following=True):
                half(i, s, own, ahead=False, following=following)
                dve.wait_ge(s_add, NPAIR * (2 * i + s) + NPAIR + 2)
                dve.sem_inc(s_settled, 1)

            edge_loop(dve, "turns_dve", loops_n, turn, s_far)
            at_end = loops_n * (2 * PER) + start0
            with dve.If(odd > 0):
                half(loops_n, 0, Steps(at_end))
                own = Steps(at_end + PER)
                last_half(loops_n, 1, own)
                last_half(loops_n + 1, 0, Steps(at_end + (PER + own.n)), following=False)
            dve.sem_inc(s_far, 1)
            with dve.If(odd < 1):
                own = Steps(at_end)
                last_half(loops_n, 0, own)
                last_half(loops_n, 1, Steps(at_end + own.n), following=False)
            dve.sem_inc(s_far, 1)
            dve.sem_inc(s_aggd, 1)

            def finish(i, s):
                dve.wait_ge(s_eb, i + 1)
                for k in range(3):
                    nb = min(3, BI - 3 * k)
                    v.tensor_tensor(apre[:, s, 3 * k:3 * k + nb],
                                    ps[:, 3 * s + k, 0:3 * (C + 1)].rearrange("p (b c) -> p b c", c=C + 1)[:, 0:nb, C],
                                    scale[:, bass.ds(BI * i + 3 * k, nb)], ALU.mult).then_inc(s_ap if k == 2 else s_ed, 1)
                dve.wait_ge(s_al, i + 1)
                v.tensor_tensor(salpha[:, s, :], alpha[:, s, :], scale[:, bass.ds(BI * i, BI)], ALU.mult).then_inc(s_ed, 1)
                dve.wait_ge(s_ed, 3 * i + 3)
                for j in range(BI):
                    to = base[:, bass.ds(BI * i + j, 1), :].rearrange("p a c -> p (a c)")
                    ins = v.scalar_tensor_tensor(out=to, in0=ps_e(s, j)[:, 0:C], scalar=salpha[:, s, j:j + 1], in1=to,
                                                 op0=ALU.mult, op1=ALU.add)
                ins.then_inc(s_fin, 1)

            dve.wait_ge(s_cn, 1)
            v.tensor_scalar(cmax[:, :], cnt_n[:, :], 1.0, None, ALU.max).then_inc(s_ec, 1)
            dve.wait_ge(s_ec, 1)
            v.reciprocal(rcnt[:, :], cmax[:, :]).then_inc(s_ec, 1)
            dve.wait_ge(s_ec, 2)
            v.tensor_tensor(scale[:, :], rcnt[:, :], a_agg[:, :], ALU.mult).then_inc(s_ec, 1)
            dve.wait_ge(s_ec, 3)
            dve.wait_ge(s_base, NI_A + 2)
            dve.wait_ge(s_base_end, NI - NI_A)
            with dve.Fori(0, (NI - 1) // 2) as i:
                finish(2 * i, 0)
                finish(2 * i + 1, 1)
            finish(NI - 1, 0)

        @block.tensor
        def _(pe):
            mm = nc.tensor.matmul
            pe.wait_ge(s_const, NCONST)
            pe.wait_ge(s_at, 32)
            nc.tensor.transpose(ps_a, at_rows[:, :], ident[0:NBLK, 0:NBLK]).then_inc(s_atT, 1)
            pe.wait_ge(s_cnt, 1)
            mm(ps_start, tri[0:ROWS, 0:ROWS], tile0_f[:, :], start=True, stop=True)
            mm(ps_total, ones[0:ROWS, :], tile0_f[:, :], start=True, stop=True).then_inc(s_pre, 1)
            pe.wait_ge(s_wdone, 5)
            def lin1(i, s):
                for j in range(BI + 1):
                    if j < BI:
                        if j == 0:
                            pe.wait_ge(s_h, i + 1)
                        pe.wait_ge(s_hT, BI * i + max(j, 1))
                        nc.tensor.transpose(ps_hT[j % 2], centred[:, s, j, :], ident[:, :]).then_inc(s_hTp, 1)
                    if j >= 1:
                        pe.wait_ge(s_hT, BI * i + j + 1)
                        pe.wait_ge(s_lsb, BI * i + max(j - 4, 0) + 1)
                        mm(ps_l[(j - 1) % 4], hT[:, j - 1, :], wl[:, :], start=True, stop=True).then_inc(s_lp, 1)
            def ids_of(c):
                first, tiles = IDS[c]
                for k in range(LCH):
                    at = P // 8 - k + first
                    last = mm(ps_id[:, 0:tiles], edge_no[:, P * k:P * (k + 1)], tile_hot[:, at:at + tiles], start=(k == 0), stop=(k == LCH - 1))
                last.then_inc(s_idp, 1)

            with pe.Fori(0, NI_A // 2) as j:
                lin1(2 * j, 0)
                lin1(2 * j + 1, 1)
            for i in range(NI_A // 2 * 2, NI_A):
                lin1(i, i % 2)
            pe.wait_ge(s_hotid, 1)
            ids_of(0)
            for i in range(NI_A, NI):
                lin1(i, i % 2)
            pe.wait_ge(s_plan, 1)
            groups_n = pe.value_load(plan[0:1, 0:1], min_val=2, max_val=GROUPS)
            loops_n = pe.value_load(plan[0:1, 1:2], min_val=0, max_val=GROUPS // 2)
            odd = pe.value_load(plan[0:1, 2:3], min_val=0, max_val=1)
            for c in range(1, len(IDS)):
                with pe.If(groups_n > IDS[c][0] // G - 4):
                    pe.wait_ge(s_ide, c)
                    ids_of(c)
            pe.wait_ge(s_lsb, NBLK + 1)

            def radial_mlp(g, s, first):
                pe.wait_ge(s_rbf, g + 1)
                nc.tensor.transpose(ps_x[0:G, P:2 * P], dst_c[:, :], ident[:, :])
                nc.tensor.transpose(ps_z[0:RBF * G, 0:P], rbf[:, :], ident[:, :]).then_inc(s_rT, 1)
                pe.wait_ge(s_rbfT, g + 1)
                for j in range(4):
                    last = mm(ps_z[:, P * j:P * (j + 1)], w1[:, j, :], rbfT[:, :], start=True, stop=True)
                last.then_inc(s_z1, 1)
                pe.wait_ge(s_h1, g + 1)
                mm(ps_z, w2[:, :], h1[:, :], start=True, stop=True).then_inc(s_z2, 1)
                pe.wait_ge(s_h2, g + 1)
                if not first:
                    pe.wait_ge(s_msg, g + 1)
                for j in range(4):
                    last = mm(ps_w[s][:, 2 * j:2 * j + 2, :], h2[:, P * j:P * (j + 1)], w3[:, :, :], start=True, stop=True)
                last.then_inc(s_w, 1)

            def spread(g):
                pe.wait_ge(s_diag, g + 1)
                mm(ps_x[:, 2 * P:2 * P + 2 * G], ones[0:G, :], diag[:, :, :], start=True, stop=True).then_inc(s_bc, 1)

            def pair_sum(q, s):
                for c in range(2):
                    for t in range(2):
                        mm(ps_s[q % 2][:, c, :], msg[:, 2 * q + t, P * c:P * (c + 1)], hot[:, s, 2 * q + t, :],
                           start=(t == 0), stop=(t == 1))
                for t in range(2):
                    last = mm(ps_s[q % 2][:, 2, :], cnt16[:, 2 * q + t, :], hot16[:, 2 * q + t, :], start=(t == 0), stop=(t == 1))
                return last

            far_turns = pe.alloc_register("far_turns_pe")
            pe.reg_mov(far_turns, 0)

            def far_windows(span, s):
                with pe.Fori(1, FAR) as k:
                    with pe.If(span >= WIN * k):
                        turn = pe.snap(far_turns)
                        pe.wait_ge(s_whot, turn + 2)
                        for q in range(NPAIR):
                            if q >= 2:
                                pe.wait_ge(s_wadd, NPAIR * turn + q)
                            pair_sum(q, s).then_inc(s_wsum, 1)
                        pe.reg_add(far_turns, far_turns, 1)

            radial_mlp(0, 0, True)
            spread(0)
            radial_mlp(1, 1, True)
            pe.wait_ge(s_ids, 1)

            def half(i, s, ahead=True, following=True):
                g = 2 * i + s
                if following:
                    spread(g + 1)
                pe.wait_ge(s_hot16, g + 1)
                pe.sem_inc(s_pe, 1)
                pe.wait_ge(s_msgc, 2 * g + 2)
                pe.sem_inc(s_pe, 1)
                span = pe.value_load(span_i[0:1, s:s + 1], min_val=0, max_val=N)
                for q in range(NPAIR):
                    pe.wait_ge(s_add, NPAIR * g + q + 1)
                    pair_sum(q, s).then_inc(s_sum, 1)
                with pe.If(span >= WIN):
                    far_windows(span, s)
                pe.sem_inc(s_pe, 1)
                if ahead:
                    radial_mlp(g + 2, s, False)

            def turn(i):
                half(i, 0)
                half(i, 1)

            edge_loop(pe, "turns_pe", loops_n, turn, s_pe)
            with pe.If(odd > 0):
                half(loops_n, 0)
                half(loops_n, 1, ahead=False)
                half(loops_n + 1, 0, ahead=False, following=False)
            pe.sem_inc(s_pe, 1)
            with pe.If(odd < 1):
                half(loops_n, 0, ahead=False)
                half(loops_n, 1, ahead=False, following=False)
            pe.sem_inc(s_pe, 1)

            def project(i, s, free):
                pe.wait_ge(s_ab, i + 1)
                if free is not None:
                    pe.wait_ge(s_fin, free)
                for j in range(BI):
                    nodes = slice(P * j, P * (j + 1))
                    for c in range(2):
                        last = mm(ps_e(s, j), aggb[s][:, c, nodes], wagg[:, c, :], start=(c == 0), stop=(c == 1))
                last.then_inc(s_eb, 1)

            project(0, 0, None)
            pe.wait_ge(s_crow, 32)
            mm(ps_a, cnt_rows[:, 0, :], ident[0:NBLK, 0:NBLK], start=True, stop=False)
            mm(ps_a, cnt_rows[:, 1, :], ident[0:NBLK, 0:NBLK], start=False, stop=True).then_inc(s_cT, 1)
            project(1, 1, None)
            with pe.Fori(0, (NI - 3) // 2) as i:
                project(2 * i + 2, 0, 2 * i + 1)
                project(2 * i + 3, 1, 2 * i + 2)
            project(NI - 1, 0, NI - 2)


_INS = ['x', 'src', 'dst', 'edge_attr_4', 'edge_weight', 'node_vec1', 'L0_gnn_sc_ws', 'L0_gnn_sc_wv', 'L0_gnn_lin1_ws',
        'L0_gnn_lin1_wv', 'L0_gnn_fc_w1', 'L0_gnn_fc_w2', 'L0_gnn_fc_w3', 'L0_gnn_lin2_ws', 'L0_gnn_lin2_wv', 'L0_gnn_alpha_w']


def kernel(**inputs):
    import concourse.bacc as bacc
    from concourse.bass_utils import run_bass_kernel_spmd

    nc = bacc.Bacc("TRN2", target_bir_lowering=False, num_devices=1)
    arrays, args = {}, []
    for name in _INS:
        a = np.ascontiguousarray(inputs[name])
        arrays[f"in_{name}"] = a
        args.append(nc.dram_tensor(f"in_{name}", a.shape, mybir.dt.from_np(a.dtype), kind="ExternalInput").ap())
    args.append(nc.dram_tensor("out_x", (N, C), F32, kind="ExternalOutput").ap())
    gnn_kernel(nc, *args)
    r = run_bass_kernel_spmd(nc, [arrays], core_ids=[0])
    return r.results[0]["out_x"]
```
